# Optimizing a Trainium2 kernel written in Bass

```python
import numpy as np
import jax
import jax.numpy as jnp

def _softmax(x, axis=-1):
    return jax.nn.softmax(x, axis=axis)

def _gelu(x):
    return jax.nn.gelu(x, approximate=True)

def _silu(x):
    return jax.nn.silu(x)

def _sigmoid(x):
    return jax.nn.sigmoid(x)

def _layernorm(x, axis=-1, eps=1e-05):
    m = jnp.mean(x, axis=axis, keepdims=True)
    v = jnp.var(x, axis=axis, keepdims=True)
    return (x - m) / jnp.sqrt(v + eps)

def _scatter_add(tgt, idx, src, axis=0):
    return tgt.at[idx].add(src)

def _segment_sum(src, seg, n):
    return jax.ops.segment_sum(src, seg, n)
kernel_name = 'mk_flamingo_gated_d1_seqx_r8_63025f'

def setup_inputs(seed: int=0):
    np.random.seed(seed)
    _w = jnp.asarray

    def _rec_inputs():
        import jax
        import jax.numpy as jnp
        _rk = jax.random.key(seed)
        x = 7.22e-05 + 1 * jax.random.normal(jax.random.fold_in(_rk, 1), (32, 64, 256), jnp.float32)
        _lenS = 64 - jax.random.randint(jax.random.fold_in(_rk, 7), (32,), 0, max(1, 64 // 4) + 1, jnp.int32)
        _lenS2 = 64 - jax.random.randint(jax.random.fold_in(_rk, 8), (32,), 0, max(1, 64 // 4) + 1, jnp.int32)
        _ctx_2048P = jax.random.normal(jax.random.fold_in(_rk, 11), (32, 16, 256), jnp.float32)
        _ctx_2048c = jax.random.dirichlet(jax.random.fold_in(_rk, 511), 0.3 * jnp.ones((16,), jnp.float32), (32, 64))
        _ctx_2048t = jnp.einsum('bsk,bkd->bsd', _ctx_2048c, _ctx_2048P)
        _ctx_2048t = _ctx_2048t * jax.lax.rsqrt(jnp.mean(jnp.square(_ctx_2048t)) + 1e-12) * 0.953939
        ctx_2048 = 4.13588e-05 + 0.999923 * (_ctx_2048t + 0.3 * jax.random.normal(jax.random.fold_in(_rk, 611), (32, 64, 256), jnp.float32))
        _g = jax.random.normal(jax.random.fold_in(_rk, 9001), (2, 1), jnp.float32)
        _g = jnp.sign(_g) * jnp.maximum(jnp.abs(_g), 1.0) + (_g == 0) * 1.0
        g_xattn = _g[0]
        g_ffn = _g[1]
        return (x, ctx_2048, g_xattn, g_ffn)
    x, ctx_2048, g_xattn, g_ffn = _rec_inputs()

    def _L0_xattn_setup():
        import jax, jax.numpy as jnp
        import numpy as np
        N_HEAD = 8
        key = jax.random.key(seed)
        k1, k2, k3 = jax.random.split(key, 3)
        b, d, m = (4, 128, 256)
        c, n = (128, 256)
        q = jax.random.normal(k1, (b, d, m), dtype=jnp.float32)
        k = jax.random.normal(k2, (d // d * b, d, n), dtype=jnp.float32).reshape(b, d, n)
        v = jax.random.normal(k3, (b, c, n), dtype=jnp.float32)
        return {'q': q, 'k': k, 'v': v}
    _L0_xattn_all = _L0_xattn_setup()
    _L0_xattn_in = {k: v for k, v in _L0_xattn_all.items() if k in ()}
    del _L0_xattn_all

    def _L0_ffn_setup():
        import jax, jax.numpy as jnp
        import numpy as np
        NUM_EXPERTS = 64
        HIDDEN = 256
        INTERMEDIATE = 128
        TOP_K = 8
        NORM_TOPK_PROB = False
        key = jax.random.key(seed)
        k1, k2, k3, k4 = jax.random.split(key, 4)
        return {'hidden_states': jax.random.normal(k1, (4, 256, HIDDEN), dtype=jnp.float32), 'router_weight': jax.random.normal(k2, (NUM_EXPERTS, HIDDEN), dtype=jnp.float32) * 0.02, 'gate_up_proj': jax.random.normal(k3, (NUM_EXPERTS, 2 * INTERMEDIATE, HIDDEN), dtype=jnp.float32) * 0.02, 'down_proj': jax.random.normal(k4, (NUM_EXPERTS, HIDDEN, INTERMEDIATE), dtype=jnp.float32) * 0.02}
    _L0_ffn_all = _L0_ffn_setup()
    _L0_ffn_in = {k: v for k, v in _L0_ffn_all.items() if k in ('router_weight', 'gate_up_proj', 'down_proj')}
    del _L0_ffn_all
    return {'x': x, 'ctx_2048': ctx_2048, 'g_xattn': g_xattn, 'g_ffn': g_ffn, 'L0_ffn_router_weight': _L0_ffn_in['router_weight'], 'L0_ffn_gate_up_proj': _L0_ffn_in['gate_up_proj'], 'L0_ffn_down_proj': _L0_ffn_in['down_proj']}

def reference(x, ctx_2048, g_xattn, g_ffn, L0_ffn_router_weight, L0_ffn_gate_up_proj, L0_ffn_down_proj):
    import jax
    import jax.numpy as jnp

    def _L0_xattn_ref(q, k, v):
        import jax, jax.numpy as jnp
        import numpy as np
        N_HEAD = 8
        b, d, m = q.shape
        c = v.shape[1]
        h = N_HEAD
        qh = q.reshape(b * h, d // h, m)
        kh = k.reshape(b * h, d // h, -1)
        vh = v.reshape(b * h, c // h, -1)
        scale = 1.0 / jnp.sqrt(jnp.asarray(d // h, dtype=q.dtype))
        qk = jnp.einsum('bdm,bdn->bmn', qh, kh) * scale
        sm = jax.nn.softmax(qk, axis=-1)
        ret = jnp.einsum('bmn,bcn->bcm', sm, vh)
        return ret.reshape(b, c, m)

    def _L0_ffn_ref(hidden_states, router_weight, gate_up_proj, down_proj):
        import jax, jax.numpy as jnp
        import numpy as np
        NUM_EXPERTS = 64
        HIDDEN = 256
        INTERMEDIATE = 128
        TOP_K = 8
        NORM_TOPK_PROB = False
        B, L, H = hidden_states.shape
        x = hidden_states.reshape(-1, H)
        T = x.shape[0]
        logits = x @ router_weight.T
        probs = jax.nn.softmax(logits.astype(jnp.float32), axis=-1)
        top_v, top_i = jax.lax.top_k(probs, TOP_K)
        if NORM_TOPK_PROB:
            top_v = top_v / jnp.sum(top_v, axis=-1, keepdims=True)
        comb = jnp.zeros((T, NUM_EXPERTS), dtype=probs.dtype)
        comb = comb.at[jnp.arange(T)[:, None], top_i].add(top_v)

        def body(acc, inputs):
            w_gu, w_d, c = inputs
            gate, up = jnp.split(x @ w_gu.T, 2, axis=-1)
            y = jax.nn.silu(gate) * up @ w_d.T
            return (acc + c[:, None] * y, None)
        out, _ = jax.lax.scan(body, jnp.zeros_like(x), (gate_up_proj, down_proj, comb.T))
        return out.reshape(B, L, H)
    x = x + jnp.tanh(g_xattn[0]) * _L0_xattn_ref(_layernorm(x, axis=-1), ctx_2048, ctx_2048)
    x = x + jnp.tanh(g_ffn[0]) * _L0_ffn_ref(_layernorm(x, axis=-1), L0_ffn_router_weight, L0_ffn_gate_up_proj, L0_ffn_down_proj)
    return x

_drawn_inputs = setup_inputs


def setup_inputs(seed=0):
    import zlib

    import numpy as np

    out = dict(_drawn_inputs(seed))
    spreads = {}
    factors = {'L0_ffn_router_weight': 8.0, 'L0_ffn_gate_up_proj': 8.0, 'L0_ffn_down_proj': 8.0}
    for name, (base, spread) in spreads.items():
        noise = np.random.default_rng([zlib.crc32(name.encode()), seed]).standard_normal(out[name].shape)
        drawn = base * np.exp(spread * noise) if base else spread * noise
        out[name] = jnp.asarray(drawn.astype(out[name].dtype))
    for name, factor in factors.items():
        out[name] = (out[name] * factor).astype(out[name].dtype)
    return out
```

```python
from contextlib import ExitStack

import concourse.bass as bass
from concourse import mybir

F32 = mybir.dt.float32
BF16 = mybir.dt.bfloat16
I32 = mybir.dt.int32
ALU = mybir.AluOpType
ACT = mybir.ActivationFunctionType
AX_X = mybir.AxisListType.X

P = 128
D = 256
B, S = 32, 64
TOK = B * S
N_HEAD = 8
HR = S // N_HEAD
TILES = TOK // P
HPT = P // HR
G = 4
J = HPT // G
MT = D // P
SCALE = float(HR) ** -0.5
EPS = 1e-5
VC = HR + 1
VW = HPT * VC + 32 - VC
E = 64
I = 128
K8 = 8
CAP = TOK + P
DUMMY = E * CAP
ROWS = DUMMY + P
GROUPS = 4
NT = -(-(TOK * K8 // P + E - 1) // GROUPS) * GROUPS
WCOLS = 2 * 2 * I + D
EXP_RING = 12
PW = 3
TAB_OPS = 23
CMB_OPS = 5 + K8
CMB2_OPS = K8 + 2
HEADS_FIRST = 7


class Turn:

    def __init__(self, i, b):
        self.i, self.b = i, b
        self.loop = not isinstance(i, int)

    def tile(self, d):
        return self.i * PW + (self.b + d)

    def slot(self, d):
        return (self.b + d) % PW

    def count(self, d, per_tile, extra):
        return self.i * (PW * per_tile) + ((self.b + d) * per_tile + extra)

    def slot_count(self, d, per_use, extra=0):
        return self.i * per_use + (((self.b + d) // PW + 1) * per_use + extra)

    def has(self, d):
        return self.loop or 0 <= self.b + d < TILES


def need(eng, sem, value):
    if isinstance(value, int) and value <= 0:
        return
    eng.wait_ge(sem, value)


def build(nc, x, keys, vals, g_attn, g_ffn, rwt, wexp, out, debug=None):
    with ExitStack() as ctx:
        def sb(name, shape, dt=F32):
            return ctx.enter_context(nc.sbuf_tensor(name, shape, dt))

        def sem(name):
            return ctx.enter_context(nc.semaphore(name))

        q_scr = nc.dram_tensor("q_scr", [PW, J * P, D], F32, kind="Internal").ap()
        o_scr = nc.dram_tensor("o_scr", [PW, J * P, D], F32, kind="Internal").ap()
        x_rows = nc.dram_tensor("x_rows", [ROWS, D], F32, kind="Internal").ap()
        y_rows = nc.dram_tensor("y_rows", [NT * P, D], F32, kind="Internal").ap()

        X = sb("X", [P, TILES + 1, D])
        XN = sb("XN", [P, PW, D])
        Q = sb("Q", [P, PW, J, D])
        K = sb("K", [P, PW, J, D])
        V = sb("V", [P, PW, MT, VW])
        PE_T = sb("PE_T", [P, EXP_RING, MT * D])
        MX = sb("MX", [P, 2, G * 2 * MT])
        MXT = sb("MXT", [G * 2 * MT, 2, P])
        O4 = sb("O4", [P, PW, J, D])
        OC = sb("OC", [P, PW, D])
        DN = sb("DN", [P, PW, D])
        OM = sb("OM", [P, PW, D])
        ST1 = sb("ST1", [P, PW, 6])
        MV1 = sb("MV1", [P, PW, 2])
        RS1 = sb("RS1", [P, PW, 1])
        ST2 = sb("ST2", [P, PW, 6])
        MV2 = sb("MV2", [P, PW, 2])
        RS2 = sb("RS2", [P, PW, 1])
        XN2 = sb("XN2", [P, PW, D])
        XT2 = sb("XT2", [P, PW, D])
        RW = sb("RW", [P, MT, E])
        NM = sb("NM", [P, PW, 1])
        EX = sb("EX", [P, PW, E])
        SE = sb("SE", [P, PW, 1])
        RSE = sb("RSE", [P, PW, 1])
        PR = sb("PR", [P, PW, E])
        TOP = sb("TOP", [P, PW, K8])
        REST = sb("REST", [P, PW, E])
        MASK = sb("MASK", [P, PW, E], BF16)
        SEEN = sb("SEEN", [P, PW, E], BF16)
        SL = sb("SL", [P, PW, E])
        SLM = sb("SLM", [P, PW, E])
        S8 = sb("S8", [P, PW, K8])
        IDX = sb("IDX", [P, PW, K8], I32)
        CMB = sb("CMB", [P, TILES, E])
        SLT = sb("SLT", [P, TILES, E])
        SLP = sb("SLP", [P, 2, E])
        TG = sb("TG", [P, 2])
        GIN = sb("GIN", [P, 2])
        IDENT = sb("IDENT", [P, P])
        UPPER = sb("UPPER", [P, P], BF16)
        ONES = sb("ONES", [P, P], BF16)
        ONESF = sb("ONESF", [E, P])
        SHIFT = sb("SHIFT", [P, E])
        NHALF = sb("NHALF", [P, 1])
        IOTI = sb("IOTI", [P, E], I32)
        BASE1 = sb("BASE1", [P, E])
        ZERO = sb("ZERO", [P, J * D])
        NI_I = sb("NI_I", [E, NT], I32)
        NI = sb("NI", [E, NT])
        EI_I = sb("EI_I", [E, 2], I32)
        EI = sb("EI", [E, 2])
        CNT = sb("CNT", [E, 8])
        CNI = sb("CNI", [E, 2], I32)
        NTB = sb("NTB", [E, 1], BF16)
        A1 = sb("A1", [E, NT])
        A2 = sb("A2", [E, NT])
        RB = sb("RB", [E, NT])
        TB = sb("TB", [E, 2 * NT + E])
        TABF = sb("TABF", [1, 2 * NT + E])
        TAB = sb("TAB", [1, 2 * NT + E], I32)
        W = sb("W", [P, GROUPS, WCOLS])
        XE = sb("XE", [P, GROUPS, D])
        XET = sb("XET", [P, 2, D])
        SG = sb("SG", [P, 2, P])
        HT = sb("HT", [P, 2, P])
        Y = sb("Y", [P, 2, D])
        YG = sb("YG", [P, 2, K8, D])
        S8C = sb("S8C", [P, 2, K8])
        IDC = sb("IDC", [P, 2, K8], I32)
        WJ = sb("WJ", [P, 2, E])
        W8 = sb("W8", [P, 2, K8])
        AC = sb("AC", [P, 2, D])
        OT = sb("OT", [P, 2, D])

        SC = ctx.enter_context(nc.psum_tensor("SC", [P, 2, 2, 512], F32))
        ST = ctx.enter_context(nc.psum_tensor("ST", [P, 3, 512], F32))
        OX = ctx.enter_context(nc.psum_tensor("OX", [P, 512], F32))

        def XP(b):
            return SC[:, 0, b, 0:D]

        def GU(b):
            return SC[:, 1, b, 0:2 * P]

        def YP(b):
            return ST[:, b, 0:D]

        x_in = sem("x_in")
        small_in = sem("small_in")
        k_in = [sem(f"k_in{n}") for n in range(PW)]
        v_in = [sem(f"v_in{n}") for n in range(PW)]
        q_zeroed = sem("q_zeroed")
        q_out = [sem(f"q_out{n}") for n in range(PW)]
        q_in = [sem(f"q_in{n}") for n in range(PW)]
        max_in = [sem(f"max_in{n}") for n in range(2)]
        o_out = [sem(f"o_out{n}") for n in range(PW)]
        o_in = [sem(f"o_in{n}") for n in range(PW)]
        dispatched = [sem(f"dispatched{n}") for n in range(PW)]
        pool_const = sem("pool_const")
        dve_const = sem("dve_const")
        tanh_done = sem("tanh_done")
        ln1 = sem("ln1")
        rstd1 = sem("rstd1")
        scored = sem("scored")
        max_done = sem("max_done")
        misc_a = sem("misc_a")
        misc_b = sem("misc_b")
        mxt_done = sem("mxt_done")
        st_done = sem("st_done")
        exp_done = sem("exp_done")
        pv_done = sem("pv_done")
        o_copied = sem("o_copied")
        att = sem("att")
        om_done = sem("om_done")
        rstd2 = sem("rstd2")
        xt_copied = sem("xt_copied")
        route = sem("route")
        rexp = sem("rexp")
        place = sem("place")
        held = [sem(f"held_{n}") for n in ("sp", "dve", "pool")]
        tab_pe = sem("tab_pe")
        tab_dve = sem("tab_dve")
        filled = sem("filled")
        w_in = [sem(f"w_in{n}") for n in range(GROUPS)]
        xe_in = [sem(f"xe_in{n}") for n in range(GROUPS)]
        xt_ps = sem("xt_ps")
        xet = sem("xet")
        gu_ps = sem("gu_ps")
        silu_done = sem("silu_done")
        h_done = sem("h_done")
        y_ps = sem("y_ps")
        y_copied = sem("y_copied")
        y_out = [sem(f"y_out{n}") for n in range(2)]
        cmb = sem("cmb")
        cmb2 = sem("cmb2")
        gathered = [sem(f"gathered{n}") for n in range(2)]
        stored = [sem(f"stored{n}") for n in range(2)]

        SP_H, DVE_H, POOL_H = held

        def hold(eng, own, s, value):
            if isinstance(value, int):
                need(eng, s, value)
            else:
                eng.wait_ge(s, value)
                eng.sem_inc(own, 1)

        def pair_s(u):
            return (0, 1) if u % 2 == 0 else (2, 3)

        def pair_t(u):
            return (2, 3) if u % 2 == 0 else (0, 1)

        HEAD_ORDER = [2, 3, 0, 1]
        UNITS = HPT // 2
        POS = {"u0": 0, "MA": 1, "u1": 2, "u2": 3, "u3": 4, "u4": 5, "MB": 6, "u5": 7, "u6": 8, "u7": 9}
        NAMES = sorted(POS, key=POS.get)

        def loaded_mid(T):
            pass

        n_full = (TILES - HEADS_FIRST) // PW

        def turns(eng, body):
            for t in range(HEADS_FIRST):
                body(Turn(0, t))
            with eng.Fori(0, n_full) as i:
                for s in range(PW):
                    body(Turn(i, HEADS_FIRST + s))
            for t in range(TILES, TILES + 4):
                body(Turn(0, t))

        block = ctx.enter_context(nc.Block())

        @block.sync
        def _(sp):
            xt = x.rearrange("(t p) d -> p t d", p=P)
            sp.dma_start(X[:, 0:2, :], xt[:, 0:2, :]).then_inc(x_in, 16)
            sp.wait_ge(dve_const, 1)
            for n in range(PW):
                sp.dma_start(q_scr[n].rearrange("(j p) d -> p j d", p=P),
                             ZERO[:, :].rearrange("p (j d) -> p j d", j=J)).then_inc(q_zeroed, 16)
            sp.dma_start(K[:, 0], keys[0]).then_inc(k_in[0], 16)
            sp.dma_start(V[:, 0], vals[0]).then_inc(v_in[0], 16)
            sp.dma_start(GIN[:, 0:1], bass.AP(g_attn.tensor, 0, [[0, P], [1, 1]])).then_inc(small_in, 16)
            sp.dma_start(GIN[:, 1:2], bass.AP(g_ffn.tensor, 0, [[0, P], [1, 1]])).then_inc(small_in, 16)
            sp.dma_start(RW[:, :, :], rwt.rearrange("(k p) e -> p k e", p=P)).then_inc(small_in, 16)

            sp.wait_ge(q_zeroed, 16 * PW)

            def q_write(T, d):
                s = T.slot(d)
                hold(sp, SP_H, ln1, T.count(d, 4, 4))
                sp.dma_start(q_scr[s].rearrange("(a r) d -> a r d", r=32)[:, 0:HR, :],
                             XN[:, s, :]).then_inc(q_out[s], 16)

            def q_read(T, d):
                s = T.slot(d)
                hold(sp, SP_H, st_done, T.count(d - 2, HPT, 0))
                hold(sp, SP_H, q_out[s], T.slot_count(d, 16))
                sp.dma_start(Q[:, s], q_scr[s].rearrange("(j p) d -> p j d", p=P)).then_inc(q_in[s], 16)

            def max_load(T, d, h):
                hold(sp, SP_H, mxt_done, T.count(d, 2, h + 1))
                sp.dma_start(Q[HR:P:32, T.slot(d), 2 * h:2 * h + 2, :],
                             MXT[:, h, :]).then_inc(max_in[h], 16)

            q_write(Turn(0, 0), 0)
            sp.wait_ge(q_out[0], 16)
            sp.dma_start(Q[:, 0], q_scr[0].rearrange("(j p) d -> p j d", p=P)).then_inc(q_in[0], 16)
            sp.dma_start(X[:, 2:TILES, :], xt[:, 2:TILES, :]).then_inc(x_in, 16)

            def turn(T):
                if T.loop or T.b < TILES:
                    s1 = T.slot(1)
                    hold(sp, SP_H, st_done, T.count(-1, HPT, 0))
                    sp.dma_start(K[:, s1], keys[bass.ds(T.tile(1), 1)] if T.loop else keys[T.b + 1]
                                 ).then_inc(k_in[s1], 16)
                if T.has(-1):
                    max_load(T, -1, 1)
                if T.has(-2):
                    s = T.slot(-2)
                    hold(sp, SP_H, o_copied, T.count(-2, J, J))
                    sp.dma_start(o_scr[s].rearrange("(j p) d -> p j d", p=P), O4[:, s]).then_inc(o_out[s], 16)
                if T.loop or T.b < TILES:
                    q_write(T, 1)
                    hold(sp, SP_H, pv_done, T.count(-1, J, 0))
                    sp.dma_start(V[:, s1], vals[bass.ds(T.tile(1), 1)] if T.loop else vals[T.b + 1]
                                 ).then_inc(v_in[s1], 16)
                if T.has(-2):
                    s = T.slot(-2)
                    hold(sp, SP_H, o_out[s], T.slot_count(-2, 16))
                    rows = o_scr[s].rearrange("(a r) d -> a r d", r=32)
                    sp.dma_start(OC[:, s, :], rows[:, 0:HR, :]).then_inc(o_in[s], 16)
                    sp.dma_start(DN[:, s, :], bass.AP(o_scr.tensor, (s * J * P + HR) * D,
                                                      [[32 * D, HPT], [0, HR], [1, D]])).then_inc(o_in[s], 16)
                if T.loop or T.b < TILES:
                    q_read(T, 1)
                if T.has(0):
                    max_load(T, 0, 0)

            turns(sp, turn)

            sp.wait_ge(tab_dve, TAB_OPS)
            sp.dma_start(x_rows[DUMMY:DUMMY + P, :], ZERO[:, 0:D]).then_inc(filled, 16)
            with sp.Fori(0, E // 2) as e:
                r = sp.value_load(TAB[0:1, bass.ds(e + 2 * NT, 1)], min_val=0, max_val=DUMMY - P)
                sp.dma_start(x_rows[bass.ds(r, P), :], ZERO[:, 0:D]).then_inc(filled, 16)
            sp.wait_ge(filled, 16 * (E + 1))
            for n in range(PW):
                sp.wait_ge(dispatched[n], 16 * K8 * len(range(n, TILES, PW)))

            def load_tile(i, n):
                at = i * GROUPS + n
                r = sp.value_load(TAB[0:1, bass.ds(at, 1)], min_val=0, max_val=DUMMY)
                e = sp.value_load(TAB[0:1, bass.ds(at + NT, 1)], min_val=0, max_val=E - 1)
                if not isinstance(i, int):
                    hold(sp, SP_H, xt_ps, at - GROUPS + 1)
                sp.dma_start(XE[:, n, :], x_rows[bass.ds(r, P), :]).then_inc(xe_in[n], 16)
                if not isinstance(i, int):
                    hold(sp, SP_H, y_ps, at - GROUPS + 1)
                sp.dma_start(W[:, n, :], wexp[bass.ds(e, 1)].rearrange("a p c -> (a p) c")).then_inc(w_in[n], 16)

            for n in range(GROUPS):
                load_tile(0, n)
            with sp.Fori(1, NT // GROUPS) as i:
                for n in range(GROUPS):
                    load_tile(i, n)

            ot = out.rearrange("(t p) d -> t p d", p=P)
            with sp.Fori(0, TILES // 2) as i:
                for s in range(2):
                    hold(sp, SP_H, cmb2, i * (2 * CMB2_OPS) + CMB2_OPS * (s + 1))
                    sp.dma_start(ot[bass.ds(i * 2 + s, 1)].rearrange("a p d -> (a p) d"), OT[:, s, :]).then_inc(stored[s], 16)
            for s in range(2):
                sp.wait_ge(stored[s], 16 * TILES // 2)

        @block.gpsimd
        def _(pool):
            nc.gpsimd.memset(IDENT[:, :], 0.0).then_inc(pool_const, 1)
            nc.gpsimd.memset(UPPER[:, :], 1.0).then_inc(pool_const, 1)
            nc.gpsimd.memset(ONES[:, :], 1.0).then_inc(pool_const, 1)
            nc.gpsimd.memset(NHALF[:, :], -0.5).then_inc(pool_const, 1)
            nc.gpsimd.iota(IOTI[:, :], pattern=[[CAP, E]], base=1, channel_multiplier=0).then_inc(pool_const, 1)
            nc.gpsimd.iota(NI_I[:, :], pattern=[[1, NT]], base=0, channel_multiplier=0).then_inc(pool_const, 1)
            nc.gpsimd.iota(EI_I[:, 0:1], pattern=[[1, 1]], base=0, channel_multiplier=1).then_inc(pool_const, 1)
            nc.gpsimd.iota(EI_I[:, 1:2], pattern=[[1, 1]], base=0, channel_multiplier=CAP).then_inc(pool_const, 1)
            pool.wait_ge(pool_const, 8)
            nc.gpsimd.affine_select(out=IDENT[:, :], in_=IDENT[:, :], compare_op=ALU.not_equal, fill=1.0, base=0,
                                    pattern=[[-1, P]], channel_multiplier=1).then_inc(pool_const, 1)
            nc.gpsimd.affine_select(out=UPPER[:, :], in_=UPPER[:, :], compare_op=ALU.is_gt, fill=0.0, base=0,
                                    pattern=[[1, P]], channel_multiplier=-1).then_inc(pool_const, 1)
            pool.wait_ge(pool_const, 10)

            def pow1(T, d):
                s = T.slot(d)
                need(pool, ln1, T.count(d, 4, 3))
                nc.gpsimd.tensor_tensor(RS1[:, s], MV1[:, s, 1:2], NHALF[:, :], ALU.pow).then_inc(rstd1, 1)

            def dispatch(T, a, b):
                if T.has(-4):
                    s = T.slot(-4)
                    if a == 0:
                        hold(pool, POOL_H, place, T.count(-4, 5, 4))
                    for k in range(a, b):
                        pool.indirect_dma_start(x_rows, bass.IndirectOffsetOnAxis(ap=IDX[:, s, k:k + 1], axis=0),
                                                XN2[:, s, :], None).then_inc(dispatched[s], 16)

            pow1(Turn(0, 0), 0)

            def turn(T):
                dispatch(T, 0, 2)
                if T.loop or T.b < TILES:
                    pow1(T, 1)
                dispatch(T, 2, 6)
                if T.has(-2):
                    s = T.slot(-2)
                    need(pool, att, T.count(-2, 6, 1))
                    nc.gpsimd.tensor_tensor(OM[:, s], OC[:, s], DN[:, s], ALU.mult).then_inc(om_done, 1)
                dispatch(T, 6, 7)
                if T.has(-2):
                    need(pool, att, T.count(-2, 6, 5))
                    nc.gpsimd.tensor_tensor(RS2[:, s], MV2[:, s, 1:2], NHALF[:, :], ALU.pow).then_inc(rstd2, 1)
                dispatch(T, 7, 8)

            turns(pool, turn)

            def store_tile(i, n):
                at = i * GROUPS + n
                hold(pool, POOL_H, y_copied, at + 1)
                pool.dma_start(y_rows[bass.ds(at * P, P), :] if not isinstance(i, int)
                               else y_rows[at * P:at * P + P, :], Y[:, n % 2, :]).then_inc(y_out[n % 2], 16)

            pool.wait_ge(tab_dve, TAB_OPS)
            for n in range(GROUPS):
                store_tile(0, n)
            with pool.Fori(1, NT // GROUPS) as i:
                for n in range(GROUPS):
                    store_tile(i, n)
            for n in range(2):
                pool.wait_ge(y_out[n], 16 * NT // 2)

            def gather(i, s):
                if not isinstance(i, int):
                    hold(pool, POOL_H, cmb2, i * (2 * CMB2_OPS) + (CMB2_OPS * (s - 2) + K8))
                hold(pool, POOL_H, cmb, i * (2 * CMB_OPS) + (CMB_OPS * s + 5))
                for k in range(K8):
                    pool.indirect_dma_start(YG[:, s, k, :], None, y_rows,
                                            bass.IndirectOffsetOnAxis(ap=IDC[:, s, k:k + 1], axis=0)
                                            ).then_inc(gathered[s], 16)

            for s in range(2):
                gather(0, s)
            with pool.Fori(1, TILES // 2) as i:
                for s in range(2):
                    gather(i, s)
            for s in range(2):
                pool.wait_ge(gathered[s], 16 * K8 * TILES // 2)

        @block.vector
        def _(dve):
            nc.vector.memset(ZERO[:, :], 0.0).then_inc(dve_const, 1)
            nc.vector.memset(X[:, TILES, :], 0.0).then_inc(dve_const, 1)
            nc.vector.memset(SEEN[:, 0, :], 0.0).then_inc(dve_const, 1)
            nc.vector.memset(ONESF[:, :], 1.0).then_inc(dve_const, 1)
            dve.wait_ge(pool_const, 8)
            nc.vector.tensor_copy(BASE1[:, :], IOTI[:, :]).then_inc(dve_const, 1)
            nc.vector.tensor_copy(NI[:, :], NI_I[:, :]).then_inc(dve_const, 1)
            nc.vector.tensor_copy(EI[:, :], EI_I[:, :]).then_inc(dve_const, 1)
            dve.wait_ge(dve_const, 7)

            def ln1_stats(T, d):
                s, at = T.slot(d), T.tile(d)
                xs = X[:, bass.ds(at, 1), :].rearrange("p a d -> p (a d)") if T.loop else X[:, at, :]
                nc.vector.bn_stats(ST1[:, s], xs).then_inc(ln1, 1)
                need(dve, ln1, T.count(d, 4, 1))
                nc.vector.bn_aggr(MV1[:, s], ST1[:, s]).then_inc(ln1, 1) if not T.loop else aggr(MV1[:, s], ST1[:, s], ln1)
                need(dve, ln1, T.count(d, 4, 2))
                nc.vector.tensor_scalar(MV1[:, s, 1:2], MV1[:, s, 1:2], EPS, None, ALU.add).then_inc(ln1, 1)

            def aggr(o, a, s):
                dve.sem_inc(DVE_H, 1)
                nc.vector.bn_aggr(o, a).then_inc(s, 1)

            def ln1_norm(T, d):
                s, at = T.slot(d), T.tile(d)
                xs = X[:, bass.ds(at, 1), :].rearrange("p a d -> p (a d)") if T.loop else X[:, at, :]
                if not (not T.loop and T.b + d < PW):
                    need(dve, q_out[s], T.slot_count(d - PW, 16))
                need(dve, rstd1, T.count(d, 1, 1))
                nc.vector.tensor_scalar(XN[:, s], xs, MV1[:, s, 0:1], RS1[:, s], ALU.subtract, ALU.mult
                                        ).then_inc(ln1, 1)

            def take_max(T, u):
                h, jj = u // 4, (u // 2) % 2
                g = pair_s(u)[0]
                pair = POS[f"u{u}"] % 2
                if u % 4 == 0:
                    need(dve, misc_b if h == 0 else misc_a, T.count(-1 if h == 0 else 0, 1, 1) if h == 0
                         else T.count(0, 1, 0))
                need(dve, scored, T.count(0, UNITS, u + 1))
                o = MX[:, h, :].rearrange("p (g j m) -> p g j m", g=G, j=2)[:, g:g + 2, jj, :]
                nc.vector.tensor_reduce(o, SC[:, pair, :, :].rearrange("p a (m n) -> p a m n", m=MT),
                                        axis=AX_X, op=ALU.max, negate=True).then_inc(max_done, 1)

            def mxt_copy(T, d, h, pair):
                need(dve, max_in[h], T.count(d - 1, 16, 16))
                nc.vector.tensor_copy(MXT[:, h, :], SC[0:16, pair, 0, 0:P]).then_inc(mxt_done, 1)

            def ma(T):
                pair = POS["MA"] % 2
                if not (T.has(-1) or T.has(-3) or T.has(-4)):
                    return
                need(dve, misc_a, T.count(0, 1, 0))
                if T.has(-1):
                    mxt_copy(T, -1, 1, pair)
                if T.has(-4):
                    s, at = T.slot(-4), T.tile(-4)
                    nc.vector.tensor_tensor(SL[:, s], SC[:, pair, 0, P:P + E], BASE1[:, :], ALU.add).then_inc(place, 1)
                if T.has(-3):
                    nc.vector.tensor_copy(XT2[:, T.slot(-3)], SC[:, pair, 1, 0:D]).then_inc(xt_copied, 1)
                if T.has(-4):
                    need(dve, place, T.count(-4, 5, 1))
                    nc.vector.tensor_tensor(SLM[:, s], SL[:, s], MASK[:, s], ALU.mult).then_inc(place, 1)
                    hold(dve, DVE_H, place, T.count(-4, 5, 2))
                    nc.vector.max(S8[:, s], SLM[:, s]).then_inc(place, 1)
                    need(dve, place, T.count(-4, 5, 3))
                    nc.vector.tensor_scalar(IDX[:, s], S8[:, s], -1.0, None, ALU.add).then_inc(place, 1)
                    a = bass.ds(at, 1) if T.loop else slice(at, at + 1)
                    nc.vector.tensor_copy(SLT[:, a, :], SLM[:, s:s + 1]).then_inc(place, 1)

            def mb(T):
                pair = POS["MB"] % 2
                if not (T.has(0) or T.has(-3)):
                    return
                need(dve, misc_b, T.count(0, 1, 1))
                if T.has(0):
                    mxt_copy(T, 0, 0, pair)
                if T.has(-3):
                    s = T.slot(-3)
                    nc.vector.tensor_reduce(NM[:, s], SC[:, pair, 1, 0:E], axis=AX_X, op=ALU.max,
                                            negate=True).then_inc(route, 1)

            def route_rest(T):
                s, at = T.slot(-3), T.tile(-3)
                need(dve, rexp, T.count(-3, 1, 1))
                nc.vector.reciprocal(RSE[:, s], SE[:, s]).then_inc(route, 1)
                need(dve, route, T.count(-3, 8, 2))
                nc.vector.tensor_scalar(PR[:, s], EX[:, s], RSE[:, s], None, ALU.mult).then_inc(route, 1)
                hold(dve, DVE_H, route, T.count(-3, 8, 3))
                nc.vector.max(TOP[:, s], PR[:, s]).then_inc(route, 1)
                hold(dve, DVE_H, route, T.count(-3, 8, 4))
                nc.vector.match_replace(REST[:, s], TOP[:, s], PR[:, s], -1.0).then_inc(route, 1)
                need(dve, route, T.count(-3, 8, 5))
                nc.vector.tensor_scalar(MASK[:, s], REST[:, s], 0.0, None, ALU.is_lt).then_inc(route, 1)
                need(dve, route, T.count(-3, 8, 6))
                a = bass.ds(at, 1) if T.loop else slice(at, at + 1)
                nc.vector.tensor_tensor(CMB[:, a, :], PR[:, s:s + 1], MASK[:, s:s + 1], ALU.mult).then_inc(route, 1)
                nc.vector.tensor_tensor(SEEN[:, T.slot(-2)], SEEN[:, s], MASK[:, s], ALU.add).then_inc(route, 1)

            def x_at(T, d):
                at = T.tile(d)
                return X[:, bass.ds(at, 1), :].rearrange("p a d -> p (a d)") if T.loop else X[:, at, :]

            def att_invert(T):
                s = T.slot(-2)
                need(dve, o_in[s], T.slot_count(-2, 32))
                nc.vector.reciprocal(DN[:, s], DN[:, s]).then_inc(att, 1)

            def att_residual(T):
                s = T.slot(-2)
                need(dve, om_done, T.count(-2, 1, 1))
                nc.vector.scalar_tensor_tensor(out=x_at(T, -2), in0=OM[:, s], scalar=TG[:, 0:1], in1=x_at(T, -2),
                                               op0=ALU.mult, op1=ALU.add).then_inc(att, 1)
                hold(dve, DVE_H, att, T.count(-2, 6, 2))
                nc.vector.bn_stats(ST2[:, s], x_at(T, -2)).then_inc(att, 1)
                hold(dve, DVE_H, att, T.count(-2, 6, 3))
                nc.vector.bn_aggr(MV2[:, s], ST2[:, s]).then_inc(att, 1)
                need(dve, att, T.count(-2, 6, 4))
                nc.vector.tensor_scalar(MV2[:, s, 1:2], MV2[:, s, 1:2], EPS, None, ALU.add).then_inc(att, 1)

            def att_norm(T):
                s = T.slot(-2)
                need(dve, rstd2, T.count(-2, 1, 1))
                if T.has(-5):
                    need(dve, dispatched[s], T.slot_count(-5, 16 * K8))
                nc.vector.tensor_scalar(XN2[:, s], x_at(T, -2), MV2[:, s, 0:1], RS2[:, s], ALU.subtract, ALU.mult
                                        ).then_inc(att, 1)

            dve.wait_ge(x_in, 16)
            ln1_stats(Turn(0, 0), 0)
            ln1_norm(Turn(0, 0), 0)
            dve.wait_ge(tanh_done, 1)

            def turn(T):
                if T.has(0):
                    take_max(T, 0)
                ma(T)
                if T.has(0):
                    take_max(T, 1)
                if T.loop or T.b < TILES:
                    if not T.loop and T.b == 1:
                        dve.wait_ge(x_in, 32)
                    ln1_stats(T, 1)
                if T.has(0):
                    take_max(T, 2)
                if T.loop or T.b < TILES:
                    ln1_norm(T, 1)
                if T.has(0):
                    take_max(T, 3)
                    take_max(T, 4)
                mb(T)
                if T.has(-2):
                    att_invert(T)
                if T.has(0):
                    take_max(T, 5)
                if T.has(-3):
                    route_rest(T)
                if T.has(0):
                    take_max(T, 6)
                if T.has(-2):
                    att_residual(T)
                if T.has(0):
                    take_max(T, 7)
                if T.has(-2):
                    att_norm(T)

            turns(dve, turn)

            n_tab = [0]

            def tab(ins, last=False):
                n_tab[0] += 1
                ins.then_inc(tab_dve, 1)
                if not last:
                    dve.wait_ge(tab_dve, n_tab[0])

            dve.wait_ge(tab_pe, 1)
            tab(nc.vector.tensor_copy(CNT[:, 0:1], SC[0:E, 0, 0, 0:1]))
            tab(nc.vector.tensor_scalar(CNI[:, 0:1], CNT[:, 0:1], float(P - 1), None, ALU.add))
            tab(nc.vector.tensor_scalar(CNI[:, 1:2], CNI[:, 0:1], 7, None, ALU.arith_shift_right))
            tab(nc.vector.tensor_copy(CNT[:, 1:2], CNI[:, 1:2]))
            tab(nc.vector.tensor_copy(NTB[:, :], CNI[:, 1:2]))
            dve.wait_ge(tab_pe, 2)
            tab(nc.vector.tensor_copy(CNT[:, 2:3], SC[0:E, 0, 1, 0:1]))
            tab(nc.vector.tensor_tensor(CNT[:, 3:4], CNT[:, 2:3], CNT[:, 1:2], ALU.add))
            tab(nc.vector.tensor_scalar(A1[:, :], NI[:, :], CNT[:, 2:3], None, ALU.is_ge))
            tab(nc.vector.tensor_scalar(A2[:, :], NI[:, :], CNT[:, 3:4], None, ALU.is_lt))
            tab(nc.vector.tensor_tensor(A1[:, :], A1[:, :], A2[:, :], ALU.mult))
            tab(nc.vector.tensor_scalar(RB[:, :], NI[:, :], CNT[:, 2:3], float(P), ALU.subtract, ALU.mult))
            tab(nc.vector.tensor_scalar(RB[:, :], RB[:, :], EI[:, 1:2], float(-DUMMY), ALU.add, ALU.add))
            tab(nc.vector.tensor_tensor(TB[:, 0:NT], RB[:, :], A1[:, :], ALU.mult))
            tab(nc.vector.tensor_scalar(TB[:, NT:2 * NT], A1[:, :], EI[:, 0:1], None, ALU.mult))
            tab(nc.vector.tensor_tensor(CNT[:, 4:5], CNT[:, 0:1], EI[:, 1:2], ALU.add))
            tab(nc.vector.tensor_scalar(TB[:, 2 * NT:2 * NT + E], IDENT[0:E, 0:E], CNT[:, 4:5], None, ALU.mult))
            tab(nc.vector.tensor_scalar(CNT[:, 5:6], CNT[:, 2:3], float(P), None, ALU.mult))
            tab(nc.vector.tensor_tensor(CNT[:, 6:7], CNT[:, 5:6], EI[:, 1:2], ALU.subtract))
            tab(nc.vector.tensor_scalar(RB[:, 0:E], IDENT[0:E, 0:E], CNT[:, 6:7], None, ALU.mult))
            dve.wait_ge(tab_pe, 3)
            tab(nc.vector.tensor_copy(TABF[:, :], SC[0:1, 1, 0, 0:2 * NT + E]))
            tab(nc.vector.tensor_copy(SHIFT[:, :], SC[:, 1, 1, 0:E]))
            tab(nc.vector.tensor_scalar(TABF[:, 0:NT], TABF[:, 0:NT], float(DUMMY), None, ALU.add))
            tab(nc.vector.tensor_copy(TAB[:, :], TABF[:, :]), last=True)
            assert n_tab[0] == TAB_OPS

            def expert(i, n):
                at = i * GROUPS + n
                b = n % 2
                if not (isinstance(i, int) and n == 0):
                    pb = (n - 1) % 2
                    need(dve, y_ps, at)
                    if not isinstance(i, int):
                        need(dve, y_out[pb], i * (16 * GROUPS // 2) + ((n - 1) // 2) * 16)
                    else:
                        need(dve, y_out[pb], ((n - 1) // 2) * 16)
                    nc.vector.tensor_copy(Y[:, pb, :], YP(pb)).then_inc(y_copied, 1)
                if n_or(i, n) is None:
                    return
                need(dve, silu_done, at + 1)
                nc.vector.tensor_tensor(HT[:, b, :], GU(b)[:, P:2 * P], SG[:, b, :], ALU.mult).then_inc(h_done, 1)

            def n_or(i, n):
                return None if isinstance(i, int) and i * GROUPS + n >= NT else n

            for n in range(GROUPS):
                expert(0, n)
            with dve.Fori(1, NT // GROUPS) as i:
                for n in range(GROUPS):
                    expert(i, n)
            need(dve, y_ps, NT)
            need(dve, y_out[1], 16 * (NT // 2 - 1))
            nc.vector.tensor_copy(Y[:, 1, :], YP(1)).then_inc(y_copied, 1)

            def weights(i, s):
                a = bass.ds(i * 2 + s, 1) if not isinstance(i, int) else slice(2 * i + s, 2 * i + s + 1)
                c0 = i * (2 * CMB_OPS) + CMB_OPS * s
                slt = SLT[:, a, :].rearrange("p a e -> p (a e)")
                pr = CMB[:, a, :].rearrange("p a e -> p (a e)")
                nc.vector.tensor_scalar(WJ[:, s], slt, 0.0, None, ALU.is_gt).then_inc(cmb, 1)
                nc.vector.tensor_tensor(SLP[:, s], slt, SHIFT[:, :], ALU.add).then_inc(cmb, 1)
                need(dve, cmb, c0 + 2)
                nc.vector.tensor_tensor(SLP[:, s], SLP[:, s], WJ[:, s], ALU.mult).then_inc(cmb, 1)
                hold(dve, DVE_H, cmb, c0 + 3)
                nc.vector.max(S8C[:, s], SLP[:, s]).then_inc(cmb, 1)
                need(dve, cmb, c0 + 4)
                nc.vector.tensor_scalar(IDC[:, s], S8C[:, s], -1.0, None, ALU.add).then_inc(cmb, 1)
                for k in range(K8):
                    need(dve, cmb, c0 + 5 + k)
                    nc.vector.scalar_tensor_tensor(out=WJ[:, s], in0=SLP[:, s], scalar=S8C[:, s, k:k + 1], in1=pr,
                                                   op0=ALU.is_equal, op1=ALU.mult,
                                                   accum_out=W8[:, s, k:k + 1]).then_inc(cmb, 1)

            def combine(i, s):
                a = bass.ds(i * 2 + s, 1) if not isinstance(i, int) else slice(2 * i + s, 2 * i + s + 1)
                c0 = i * (2 * CMB2_OPS) + CMB2_OPS * s
                need(dve, gathered[s], i * (16 * K8) + 16 * K8)
                nc.vector.tensor_scalar(AC[:, s], YG[:, s, 0, :], W8[:, s, 0:1], None, ALU.mult).then_inc(cmb2, 1)
                for k in range(1, K8):
                    need(dve, cmb2, c0 + k)
                    nc.vector.scalar_tensor_tensor(out=AC[:, s], in0=YG[:, s, k, :], scalar=W8[:, s, k:k + 1],
                                                   in1=AC[:, s], op0=ALU.mult, op1=ALU.add).then_inc(cmb2, 1)
                need(dve, cmb2, c0 + K8)
                nc.vector.tensor_scalar(AC[:, s], AC[:, s], TG[:, 1:2], None, ALU.mult).then_inc(cmb2, 1)
                need(dve, stored[s], i * 16)
                need(dve, cmb2, c0 + K8 + 1)
                nc.vector.tensor_tensor(OT[:, s:s + 1], AC[:, s:s + 1], X[:, a, :], ALU.add).then_inc(cmb2, 1)

            for s in range(2):
                weights(0, s)
            for s in range(2):
                combine(0, s)
                weights(1, s)
            with dve.Fori(1, TILES // 2 - 1) as i:
                for s in range(2):
                    combine(i, s)
                    weights(i + 1, s)
            for s in range(2):
                combine(TILES // 2 - 1, s)

        @block.scalar
        def _(act):
            act.wait_ge(small_in, 48)
            nc.scalar.activation(TG[:, :], GIN[:, :], ACT.Tanh).then_inc(tanh_done, 1)

            def turn(T):
                for u in range(UNITS):
                    if T.has(-1):
                        for a in range(2):
                            n = 2 * u + a
                            h = HPT * (T.b - 1) + n
                            if n % 4 == 0:
                                need(act, pv_done, T.count(-1, J, n // 4 - EXP_RING // 4 + 1))
                            need(act, st_done, T.count(-1, HPT, n + 1))
                            nc.scalar.activation(PE_T[:, h % EXP_RING, :], ST[:, h % 3, :], ACT.Exp,
                                                 scale=SCALE).then_inc(exp_done, 1)
                    if u == 5 and T.has(-3):
                        s = T.slot(-3)
                        need(act, route, T.count(-3, 8, 1))
                        nc.scalar.activation(EX[:, s], SC[:, POS["MB"] % 2, 1, 0:E], ACT.Exp, bias=NM[:, s],
                                             accum_out=SE[:, s]).then_inc(rexp, 1)
                    if u % 2 == 1:
                        d, j = (-2, 3) if u == 1 else (-1, (u - 3) // 2)
                        if T.has(d):
                            s = T.slot(d)
                            if j == 0:
                                if T.loop or T.b + d - PW >= 0:
                                    need(act, o_out[s], T.slot_count(d - PW, 16))
                            need(act, pv_done, T.count(d, J, j + 1))
                            nc.scalar.copy(O4[:, s, j, :], OX[:, 0:D]).then_inc(o_copied, 1)

            turns(act, turn)

            act.wait_ge(tab_dve, TAB_OPS)
            with act.Fori(0, E // 2) as e:
                r = act.value_load(TAB[0:1, bass.ds(e + (2 * NT + E // 2), 1)], min_val=0, max_val=DUMMY - P)
                act.dma_start(x_rows[bass.ds(r, P), :], ZERO[:, 0:D]).then_inc(filled, 16)

            def expert(i, n):
                at = i * GROUPS + n
                b = n % 2
                if not (isinstance(i, int) and n < 2):
                    need(act, h_done, at - 1)
                need(act, gu_ps, at + 1)
                nc.scalar.activation(SG[:, b, :], GU(b)[:, 0:P], ACT.Silu).then_inc(silu_done, 1)

            def xt(i, n):
                at = i * GROUPS + n
                b = n % 2
                need(act, xt_ps, at + 1)
                if not (isinstance(i, int) and at < 2):
                    need(act, gu_ps, at - 1)
                nc.scalar.copy(XET[:, b, :], XP(b)).then_inc(xet, 1)

            xt(0, 0)
            for n in range(GROUPS):
                xt(0, n + 1)
                expert(0, n)
            with act.Fori(1, NT // GROUPS - 1) as i:
                for n in range(GROUPS):
                    xt(i, n + 1)
                    expert(i, n)
            for n in range(GROUPS):
                if n + 1 < GROUPS:
                    xt(NT // GROUPS - 1, n + 1)
                expert(NT // GROUPS - 1, n)

        @block.tensor
        def _(pe):
            pe.wait_ge(pool_const, 10)
            pe.wait_ge(small_in, 48)

            def slot_free(T, name):
                at = POS[name] - 2
                d = 0
                if at < 0:
                    at, d = at + len(NAMES), -1
                before = NAMES[at]
                if before == "MA":
                    if T.has(d - 1):
                        need(pe, mxt_done, T.count(d - 1, 2, 2))
                    if T.has(d - 3):
                        need(pe, xt_copied, T.count(d - 3, 1, 1))
                    if T.has(d - 4):
                        need(pe, place, T.count(d - 4, 5, 1))
                elif before == "MB":
                    if T.has(d):
                        need(pe, mxt_done, T.count(d, 2, 1))
                    if T.has(d - 3):
                        need(pe, rexp, T.count(d - 3, 1, 1))
                elif T.has(d):
                    need(pe, max_done, T.count(d, UNITS, int(before[1]) + 1))

            def step(T, u):
                j = u // 2
                s0, s1 = T.slot(0), T.slot(-1)
                if T.has(0):
                    if u == 0:
                        need(pe, k_in[s0], T.slot_count(0, 16))
                        need(pe, q_in[s0], T.slot_count(0, 16))
                    slot_free(T, f"u{u}")
                if T.has(-1):
                    if u % 4 == 0:
                        need(pe, max_in[u // 4], T.count(-1, 16, 16))
                    need(pe, exp_done, T.count(-1, HPT, 2 * u - 1))
                pair = POS[f"u{u}"] % 2
                for r in range(MT):
                    if T.has(0):
                        for a, g in enumerate(pair_s(u)):
                            rows = slice(32 * g, 32 * g + HR)
                            mm = nc.tensor.matmul(SC[:, pair, a, r * D:(r + 1) * D],
                                                  Q[rows, s0, j, r * P:(r + 1) * P], K[rows, s0, j, :],
                                                  start=True, stop=True)
                            if r == 1 and a == 1:
                                mm.then_inc(scored, 1)
                    if T.has(-1):
                        for a, g in enumerate(pair_t(u)):
                            rows = slice(32 * g, 32 * g + HR + 1)
                            bank = (HPT * (T.b - 1) + 2 * u + a) % 3
                            mm = nc.tensor.matmul(ST[:, bank, r * D:(r + 1) * D],
                                                  K[rows, s1, j, r * P:(r + 1) * P], Q[rows, s1, j, :],
                                                  start=True, stop=True)
                            if r == 1:
                                mm.then_inc(st_done, 1)

            def sums(T, d, j):
                s = T.slot(d)
                if j == 0:
                    need(pe, v_in[s], T.slot_count(d, 16))
                need(pe, exp_done, T.count(d, HPT, 4 * j + 4))
                need(pe, o_copied, T.count(d, J, j))
                for r in range(MT):
                    for a, g in enumerate(HEAD_ORDER):
                        h = HPT * (T.b + d) + 4 * j + a
                        c = (4 * j + g) * VC
                        mm = nc.tensor.matmul(OX[32 * g:32 * g + 32, 0:D], V[:, s, r, c:c + 32],
                                              PE_T[:, h % EXP_RING, r * D:(r + 1) * D],
                                              start=(r == 0), stop=(r == 1))
                mm.then_inc(pv_done, 1)

            def ma(T):
                if not (T.has(-1) or T.has(-3) or T.has(-4)):
                    return
                slot_free(T, "MA")
                pair = POS["MA"] % 2
                mm = None
                if T.has(-1):
                    need(pe, max_done, T.count(-1, UNITS, UNITS))
                    mm = nc.tensor.transpose(SC[0:16, pair, 0, 0:P], MX[:, 1, :], IDENT[:, :])
                if T.has(-4):
                    s = T.slot(-4)
                    need(pe, route, T.count(-4, 8, 8))
                    nc.tensor.matmul(SC[:, pair, 0, P:P + E], UPPER[:, :], MASK[:, s], start=True, stop=False)
                    mm = nc.tensor.matmul(SC[:, pair, 0, P:P + E], ONES[:, :], SEEN[:, s], start=False, stop=True)
                if T.has(-3):
                    s = T.slot(-3)
                    need(pe, att, T.count(-3, 6, 6))
                    for k in range(MT):
                        mm = nc.tensor.transpose(SC[:, pair, 1, k * P:(k + 1) * P], XN2[:, s, k * P:(k + 1) * P],
                                                 IDENT[:, :])
                mm.then_inc(misc_a, 1)

            def mb(T):
                if not (T.has(0) or T.has(-3)):
                    return
                slot_free(T, "MB")
                pair = POS["MB"] % 2
                if T.has(0):
                    need(pe, max_done, T.count(0, UNITS, 4))
                    mm = nc.tensor.transpose(SC[0:16, pair, 0, 0:P], MX[:, 0, :], IDENT[:, :])
                if T.has(-3):
                    s = T.slot(-3)
                    need(pe, xt_copied, T.count(-3, 1, 1))
                    for k in range(MT):
                        mm = nc.tensor.matmul(SC[:, pair, 1, 0:E], XT2[:, s, k * P:(k + 1) * P], RW[:, k, :],
                                              start=(k == 0), stop=(k == MT - 1))
                mm.then_inc(misc_b, 1)

            def turn(T):
                for u in range(UNITS):
                    step(T, u)
                    if u == 0:
                        ma(T)
                    if u == 4:
                        mb(T)
                    if u == 1 and T.has(-2):
                        sums(T, -2, 3)
                    if u in (3, 5, 7) and T.has(-1):
                        sums(T, -1, (u - 3) // 2)

            turns(pe, turn)

            last = TILES % PW
            pe.wait_ge(route, 8 * TILES)
            pe.wait_ge(place, 5 * TILES)
            nc.tensor.matmul(SC[0:E, 0, 0, 0:1], SEEN[:, last], ONES[:, 0:1], start=True, stop=True
                             ).then_inc(tab_pe, 1)
            pe.wait_ge(tab_dve, 5)
            nc.tensor.matmul(SC[0:E, 0, 1, 0:1], UPPER[0:E, 0:E], NTB[:, :], start=True, stop=True
                             ).then_inc(tab_pe, 1)
            pe.wait_ge(tab_dve, TAB_OPS - 4)
            nc.tensor.matmul(SC[0:1, 1, 0, 0:2 * NT + E], ONESF[:, 0:1], TB[:, :], start=True, stop=True)
            nc.tensor.matmul(SC[:, 1, 1, 0:E], ONESF[:, :], RB[:, 0:E], start=True, stop=True
                             ).then_inc(tab_pe, 1)

            def rows_t(i, n):
                at = i * GROUPS + n
                b, s = n % 2, n % GROUPS
                use = i + n // GROUPS
                need(pe, xe_in[s], use * 16 + 16)
                if not (isinstance(i, int) and at < 2):
                    need(pe, xet, at - 1)
                for k in range(MT):
                    mm = nc.tensor.transpose(XP(b)[:, k * P:(k + 1) * P], XE[:, s, k * P:(k + 1) * P], IDENT[:, :])
                mm.then_inc(xt_ps, 1)

            def gate_up(i, n):
                at = i * GROUPS + n
                b = n % 2
                need(pe, xet, at + 1)
                need(pe, w_in[n], i * 16 + 16)
                if not (isinstance(i, int) and at < 2):
                    need(pe, h_done, at - 1)
                for c in range(2):
                    for k in range(MT):
                        mm = nc.tensor.matmul(GU(b)[:, c * P:(c + 1) * P],
                                              W[:, n, k * 2 * I + c * I:k * 2 * I + (c + 1) * I],
                                              XET[:, b, k * P:(k + 1) * P], start=(k == 0), stop=(k == MT - 1))
                mm.then_inc(gu_ps, 1)

            def down(i, n):
                at = i * GROUPS + n
                b, s = n % 2, n % GROUPS
                need(pe, h_done, at + 1)
                if not (isinstance(i, int) and at < 2):
                    need(pe, y_copied, at - 1)
                nc.tensor.matmul(YP(b), HT[:, b, :], W[:, s, 4 * I:], start=True, stop=True).then_inc(y_ps, 1)

            pe.wait_ge(tab_dve, TAB_OPS)
            rows_t(0, 0)
            for n in range(GROUPS):
                rows_t(0, n + 1)
                gate_up(0, n)
                if n:
                    down(0, n - 1)
            with pe.Fori(1, NT // GROUPS - 1) as i:
                for n in range(GROUPS):
                    rows_t(i, n + 1)
                    gate_up(i, n)
                    down(i, n - 1)
            last = NT // GROUPS - 1
            for n in range(GROUPS):
                if n + 1 < GROUPS:
                    rows_t(last, n + 1)
                gate_up(last, n)
                down(last, n - 1)
            down(last, GROUPS - 1)


def kernel(x, ctx_2048, g_xattn, g_ffn, L0_ffn_router_weight, L0_ffn_gate_up_proj, L0_ffn_down_proj):
    import numpy as np
    import concourse.bacc as bacc
    from concourse.bass_utils import run_bass_kernel_spmd as run

    f = np.float32
    rows = np.ascontiguousarray(x).reshape(TOK, D)
    ctx = np.ascontiguousarray(ctx_2048).reshape(TILES, J, G, HR, D)
    keys = np.zeros((TILES + 1, G, 32, J, D), f)
    keys[:TILES, :, :HR] = ctx.transpose(0, 2, 3, 1, 4)
    keys[:, :, HR] = 1.0
    vals = np.ones((TILES + 1, P, MT, VW), f)
    ctx_t = np.ascontiguousarray(ctx_2048).reshape(TILES, HPT, HR, MT, P).transpose(0, 4, 3, 1, 2)
    vals[:TILES, :, :, :HPT * VC].reshape(TILES, P, MT, HPT, VC)
    heads = np.ones((TILES, P, MT, HPT, VC), f)
    heads[..., :HR] = ctx_t
    vals[:TILES, :, :, :HPT * VC] = heads.reshape(TILES, P, MT, HPT * VC)
    gu = np.ascontiguousarray(L0_ffn_gate_up_proj).reshape(E, 2 * I, MT, P).transpose(0, 3, 2, 1).reshape(E, P, 4 * I)
    dn = np.ascontiguousarray(L0_ffn_down_proj).transpose(0, 2, 1)
    arrays = {
        "x_in_dram": rows,
        "keys_dram": keys.reshape(TILES + 1, P, J, D),
        "vals_dram": vals,
        "g_attn_dram": np.ascontiguousarray(g_xattn).reshape(1),
        "g_ffn_dram": np.ascontiguousarray(g_ffn).reshape(1),
        "router_dram": np.ascontiguousarray(np.asarray(L0_ffn_router_weight).T),
        "experts_dram": np.ascontiguousarray(np.concatenate([gu, dn], axis=2)),
    }
    nc = bacc.Bacc("TRN2", target_bir_lowering=False, num_devices=1)
    aps = [nc.dram_tensor(n, a.shape, F32, kind="ExternalInput").ap() for n, a in arrays.items()]
    out = nc.dram_tensor("out_dram", (TOK, D), F32, kind="ExternalOutput").ap()
    build(nc, *aps, out)
    r = run(nc, [arrays], core_ids=[0])
    return r.results[0]["out_dram"].reshape(B, S, D)
```

```python
from contextlib import ExitStack

import concourse.bass as bass
from concourse import mybir

F32 = mybir.dt.float32
BF16 = mybir.dt.bfloat16
F32R = mybir.dt.float32r
I32 = mybir.dt.int32
ALU = mybir.AluOpType
ACT = mybir.ActivationFunctionType
AX_X = mybir.AxisListType.X

P = 128
D = 256
B, S = 32, 64
TOK = B * S
N_HEAD = 8
HR = S // N_HEAD
TILES = TOK // P
HPT = P // HR
G = 4
J = HPT // G
MT = D // P
SCALE = float(HR) ** -0.5
EPS = 1e-5
VC = HR + 1
VW = HPT * VC + 32 - VC
E = 64
I = 128
K8 = 8
CAP = TOK + P
MAIN = 320
ROWS_J = (P, P, MAIN - 2 * P)
NJ = len(ROWS_J)
ROW = D + E + 1
DUMMY = E * CAP
SLOTS = 8
FS = 4
NO = max(k * (min(TOK, TOK * K8 // k) - MAIN + P - 1) // P for k in range(1, E + 1) if TOK * K8 // k > MAIN)
WCOLS = 2 * 2 * I + D
EXP_RING = 12
PW = 3
TAB_OPS = 21
TAB_N = 2 * NO + E + 1
HEADS_FIRST = 7


class Turn:

    def __init__(self, i, b):
        self.i, self.b = i, b
        self.loop = not isinstance(i, int)

    def tile(self, d):
        return self.i * PW + (self.b + d)

    def slot(self, d):
        return (self.b + d) % PW

    def count(self, d, per_tile, extra):
        return self.i * (PW * per_tile) + ((self.b + d) * per_tile + extra)

    def slot_count(self, d, per_use, extra=0):
        return self.i * per_use + (((self.b + d) // PW + 1) * per_use + extra)

    def has(self, d):
        return self.loop or 0 <= self.b + d < TILES


def need(eng, sem, value):
    if isinstance(value, int) and value <= 0:
        return
    eng.wait_ge(sem, value)


PARTS = 2
QK = PARTS * PARTS * HR
MAXR = 96
LAST = 5


def build(nc, x, keys, vals, g_attn, g_ffn, rwt, wexp, out, debug=None):
    with ExitStack() as ctx:
        def sb(name, shape, dt=F32):
            return ctx.enter_context(nc.sbuf_tensor(name, shape, dt))

        def sem(name):
            return ctx.enter_context(nc.semaphore(name))

        q_scr = nc.dram_tensor("q_scr", [PW, PARTS, HR, HPT * D], F32, kind="Internal").ap()
        k_scr = nc.dram_tensor("k_scr", [PW, PARTS, HR, HPT * D], F32, kind="Internal").ap()
        r_scr = nc.dram_tensor("r_scr", [PW, HPT, D], F32, kind="Internal").ap()
        o_scr = nc.dram_tensor("o_scr", [PW, J * P, D], F32, kind="Internal").ap()
        x_rows = nc.dram_tensor("x_rows", [DUMMY + P, ROW], F32, kind="Internal").ap()
        sums_dram = [nc.dram_tensor(f"sums{j}", [TOK + P, D], F32, kind="Internal").ap() for j in range(NJ)]

        X = sb("X", [P, TILES + 2, D])
        SHARED = sb("SHARED", [P, 5 * PW * D])

        def shared(at, n, d):
            return SHARED[:, at:at + n * d].rearrange("p (n d) -> p n d", d=d)

        XN = shared(0, PW, D)
        QS = sb("QS", [P, PW, PARTS, D], F32R)
        KR = shared(1 * PW * D, PW, D)
        KS = sb("KS", [P, PW, PARTS, D], F32R)
        V = sb("V", [P, PW, MT, VW])
        PE_T = sb("PE_T", [P, EXP_RING, MT * D])
        MX = sb("MX", [P, 2, HPT // 2 * MT])
        MXT = sb("MXT", [HPT // 2 * MT, 2, PARTS, P], F32R)
        O4 = sb("O4", [P, PW, J, D])
        OC = shared(2 * PW * D, PW, D)
        SM = sb("SM", [P, PW, HPT * D // P])
        DN = shared(3 * PW * D, PW, D)
        OM = shared(4 * PW * D, PW, D)
        ST1 = sb("ST1", [P, PW, 6])
        MV1 = sb("MV1", [P, PW, 2])
        RS1 = sb("RS1", [P, PW, 2])
        ST2 = sb("ST2", [P, PW, 6])
        MV2 = sb("MV2", [P, PW, 2])
        RS2 = sb("RS2", [P, PW, 2])
        XN2 = sb("XN2", [P, PW, ROW])
        XT2 = sb("XT2", [P, PW, D])
        RW = sb("RW", [P, MT, E])
        NM = sb("NM", [P, PW, 1])
        EX = sb("EX", [P, PW, E])
        SE = sb("SE", [P, PW, 1])
        RSE = sb("RSE", [P, PW, 1])
        PR = sb("PR", [P, PW, E])
        TOP = sb("TOP", [P, PW, K8])
        REST = sb("REST", [P, PW, E])
        MASK = sb("MASK", [P, PW, E], BF16)
        SEEN = sb("SEEN", [P, PW, E], BF16)
        SL = sb("SL", [P, PW, E])
        SLM = sb("SLM", [P, PW, E])
        S8 = sb("S8", [P, PW, K8])
        IDX = sb("IDX", [P, PW, K8], I32)
        TG = sb("TG", [P, 2])
        GIN = sb("GIN", [P, 2])
        IDENT = sb("IDENT", [P, P])
        UPPER = sb("UPPER", [P, P], BF16)
        ONES = sb("ONES", [P, P], BF16)
        ONESF = sb("ONESF", [E, P])
        NHALF = sb("NHALF", [P, 1])
        IOTI = sb("IOTI", [P, E], I32)
        BASE1 = sb("BASE1", [P, E])
        ZERO = sb("ZERO", [P, D])
        FILL = sb("FILL", [P, 2, ROW])
        TOKEN = sb("TOKEN", [P, TILES], I32)
        NI_I = sb("NI_I", [E, NO], I32)
        NI = sb("NI", [E, NO])
        EI_I = sb("EI_I", [E, 2], I32)
        EI = sb("EI", [E, 2])
        CNT = sb("CNT", [E, 8])
        CNI = sb("CNI", [E, 2], I32)
        NTB = sb("NTB", [E, 1], BF16)
        A1 = PE_T[0:E, 8, 0:NO]
        A2 = PE_T[0:E, 8, NO:2 * NO]
        RB = PE_T[0:E, 9, 0:NO]
        TB = PE_T[0:E, 10, 0:TAB_N]
        TABF = PE_T[0:1, 11, 0:TAB_N]
        TAB = PE_T[0:1, 8, 0:TAB_N].bitcast(I32)
        EXPS = PE_T.rearrange("p a b -> p (a b)")

        def exps(at, n, d):
            return EXPS[:, at:at + n * d].rearrange("p (n d) -> p n d", d=d)

        XET = exps(0, 2 * MT, MAIN).rearrange("p (b k) m -> p b k m", k=MT)
        SG = exps(2 * MT * MAIN, 2, MAIN)
        HT = exps(2 * MT * MAIN + 2 * MAIN, 2, MAIN)
        Y = exps(2 * MT * MAIN + 4 * MAIN, 2 * NJ, D).rearrange("p (b j) d -> p b j d", j=NJ)
        ACC = SHARED[:, 0:FS * NJ * D].rearrange("p (n j d) -> p n j d", j=NJ, d=D)
        OT = exps(0, FS, D)

        with ExitStack() as attention:
            Q = attention.enter_context(nc.sbuf_tensor("Q", [MAXR + PARTS, PW, HPT, D], F32R))
            K = attention.enter_context(nc.sbuf_tensor("K", [MAXR + PARTS, PW, HPT, D], F32R))
        W = sb("W", [P, SLOTS, WCOLS])
        XE = sb("XE", [P, SLOTS, NJ, ROW])

        SC = ctx.enter_context(nc.psum_tensor("SC", [P, 2, 2, 512], F32))
        ST = ctx.enter_context(nc.psum_tensor("ST", [P, 3, 512], F32))
        OX = ctx.enter_context(nc.psum_tensor("OX", [P, 512], F32))

        XP = ST[:, 0:MT, 0:MAIN]
        GU = SC[:, :, :, 0:MAIN]
        YP = [ST[:, 2, 0:D], ST[:, 2, D:2 * D], OX[:, 0:D]]

        x_in = sem("x_in")
        gates_in = sem("gates_in")
        router_in = sem("router_in")
        kr_in = [sem(f"kr_in{n}") for n in range(PW)]
        k_out = [sem(f"k_out{n}") for n in range(PW)]
        k_in = [sem(f"k_in{n}") for n in range(PW)]
        v_in = [sem(f"v_in{n}") for n in range(PW)]
        q_out = [sem(f"q_out{n}") for n in range(PW)]
        q_in = [sem(f"q_in{n}") for n in range(PW)]
        max_in = [sem(f"max_in{n}") for n in range(2)]
        o_out = [sem(f"o_out{n}") for n in range(PW)]
        o_in = [sem(f"o_in{n}") for n in range(PW)]
        s_in = [sem(f"s_in{n}") for n in range(PW)]
        r_out = [sem(f"r_out{n}") for n in range(PW)]
        r_in = [sem(f"r_in{n}") for n in range(PW)]
        dispatched = [sem(f"dispatched{n}") for n in range(PW)]
        pool_const = sem("pool_const")
        dve_const = sem("dve_const")
        q_zero = sem("q_zero")
        k_zero = sem("k_zero")
        k_ones = sem("k_ones")
        tanh_done = sem("tanh_done")
        ln1 = sem("ln1")
        rstd1 = sem("rstd1")
        norm1 = sem("norm1")
        k_high = sem("k_high")
        k_low = sem("k_low")
        scored = sem("scored")
        max_done = sem("max_done")
        misc_a = sem("misc_a")
        misc_b = sem("misc_b")
        mxt_high = sem("mxt_high")
        mxt_low = sem("mxt_low")
        st_done = sem("st_done")
        exp_done = sem("exp_done")
        pv_done = sem("pv_done")
        o_copied = sem("o_copied")
        inverted = sem("inverted")
        att = sem("att")
        om_done = sem("om_done")
        rstd2 = sem("rstd2")
        norm2 = sem("norm2")
        xt_copied = sem("xt_copied")
        route = sem("route")
        rexp = sem("rexp")
        place = sem("place")
        held = [sem(f"held_{n}") for n in ("sp", "dve", "pool", "act")]
        tab_pe = sem("tab_pe")
        tab_dve = sem("tab_dve")
        filled = [sem(f"filled{c}") for c in range(3)]
        sums_zero = sem("sums_zero")
        w_in = [sem(f"w_in{n}") for n in range(SLOTS)]
        xe_in = [sem(f"xe_in{n}") for n in range(SLOTS)]
        xt_ps = sem("xt_ps")
        xet = sem("xet")
        gu_ps = sem("gu_ps")
        silu_done = sem("silu_done")
        h_done = sem("h_done")
        y_ps = sem("y_ps")
        y_weighted = sem("y_weighted")
        added = [sem(f"added{j}") for j in range(NJ)]
        o_free = sem("o_free")
        o_fill = sem("o_fill")
        o_loaded = sem("o_loaded")
        o_xt_ps = sem("o_xt_ps")
        o_xet = sem("o_xet")
        o_gu_ps = sem("o_gu_ps")
        o_silu = sem("o_silu")
        o_h = sem("o_h")
        o_y_ps = sem("o_y_ps")
        o_weighted = sem("o_weighted")
        o_added = sem("o_added")
        acc_in = [sem(f"acc_in{n}") for n in range(FS)]
        summed = sem("summed")
        stored = [sem(f"stored{n}") for n in range(FS)]

        SP_H, DVE_H, POOL_H, ACT_H = held

        def hold(eng, own, s, value):
            if isinstance(value, int):
                need(eng, s, value)
            else:
                eng.wait_ge(s, value)
                eng.sem_inc(own, 1)

        FILLS = 2 * E // 8 + E // 16 + 1
        UNITS = HPT // 2
        POS = {"u0": 0, "MA": 1, "u1": 2, "u2": 3, "u3": 4, "u4": 5, "MB": 6, "u5": 7, "u6": 8, "u7": 9}
        NAMES = sorted(POS, key=POS.get)

        def ahead(T):
            return T.loop or T.b < TILES

        n_full = (TILES - HEADS_FIRST) // PW
        assert n_full * PW == TILES - HEADS_FIRST

        def turns(eng, body):
            for t in range(HEADS_FIRST):
                body(Turn(0, t))
            with eng.Fori(0, n_full) as i:
                for s in range(PW):
                    body(Turn(i, HEADS_FIRST + s))
            for t in range(TILES, TILES + LAST):
                body(Turn(0, t))

        block = ctx.enter_context(nc.Block())

        @block.sync
        def _(sp):
            xt = x.rearrange("(t p) d -> p t d", p=P)
            sp.dma_start(X[:, 0:2, :], xt[:, 0:2, :]).then_inc(x_in, 16)
            sp.dma_start(KR[:, 0], keys[0]).then_inc(kr_in[0], 16)
            sp.dma_start(KR[:, 1], keys[1]).then_inc(kr_in[1], 16)
            sp.dma_start(KR[:, 2], keys[2]).then_inc(kr_in[2], 16)
            sp.dma_start(GIN[:, 0:1], bass.AP(g_attn.tensor, 0, [[0, P], [1, 1]])).then_inc(gates_in, 16)
            sp.dma_start(GIN[:, 1:2], bass.AP(g_ffn.tensor, 0, [[0, P], [1, 1]])).then_inc(gates_in, 16)

            def part_write(T, d, scr, parts, out_sem, ready, per_tile):
                s = T.slot(d)
                hold(sp, SP_H, ready, T.count(d, per_tile, per_tile))
                sp.dma_start(scr[s].rearrange("a c (n d) -> a (c n) d", d=D).rearrange("a p d -> p a d"),
                             parts[:, s].bitcast(F32)).then_inc(out_sem[s], 16)

            def rows_zeroed(T, d, zeroed):
                if not T.loop and T.b + d < PW:
                    sp.wait_ge(zeroed, T.b + d + 1)

            def q_read(T, d):
                s = T.slot(d)
                rows_zeroed(T, d, q_zero)
                hold(sp, SP_H, st_done, T.count(d - 2, HPT, 0))
                hold(sp, SP_H, q_out[s], T.slot_count(d, 16))
                for n in range(2):
                    sp.dma_start(Q[16 * n:16 * n + 16, s].bitcast(F32).rearrange("p n d -> p (n d)"),
                                 q_scr[s].rearrange("a c m -> (a c) m")).then_inc(q_in[s], 16)

            def k_read(T, d):
                s = T.slot(d)
                rows_zeroed(T, d, k_zero)
                hold(sp, SP_H, st_done, T.count(d - 2, HPT, 0))
                hold(sp, SP_H, k_out[s], T.slot_count(d, 16))
                rows = k_scr[s].rearrange("a c m -> (a c) m")
                for to, of, n in ((0, 0, 16), (16, 8, 8), (24, 0, 8)):
                    sp.dma_start(K[to:to + n, s].bitcast(F32).rearrange("p n d -> p (n d)"), rows[of:of + n, :]
                                 ).then_inc(k_in[s], 16)

            def max_load(T, d, h):
                hold(sp, SP_H, mxt_low, T.count(d, 2, h + 1))
                for a in range(PARTS):
                    sp.dma_start(Q[MAXR + a:MAXR + a + 1, T.slot(d), HPT // 2 * h:HPT // 2 * (h + 1), :].bitcast(F32),
                                 MXT[:, h, a, :].bitcast(F32)).then_inc(max_in[h], 16)

            sp.wait_ge(dve_const, 4)
            sp.dma_start(K[MAXR:].bitcast(F32).rearrange("p s n d -> p (s n d)"),
                         bass.AP(ONESF[:, :].tensor, 0, [[P, PARTS], [0, PW * HPT * D // P], [1, P]])).then_inc(k_ones, 16)
            T0 = Turn(0, 0)
            part_write(T0, 0, k_scr, KS, k_out, k_low, 1)
            part_write(T0, 0, q_scr, QS, q_out, ln1, 4)
            k_read(T0, 0)
            q_read(T0, 0)
            part_write(T0, 1, k_scr, KS, k_out, k_low, 1)
            part_write(T0, 1, q_scr, QS, q_out, ln1, 4)
            sp.dma_start(V[:, 0], vals[0]).then_inc(v_in[0], 16)
            sp.dma_start(RW[:, :, :], rwt.rearrange("(k p) e -> p k e", p=P)).then_inc(router_in, 16)
            sp.dma_start(X[:, 2:TILES, :], xt[:, 2:TILES, :]).then_inc(x_in, 16)

            def turn(T):
                if ahead(T):
                    k_read(T, 1)
                    q_read(T, 1)
                    s3 = T.slot(3)
                    hold(sp, SP_H, k_low, T.count(1, 1, 0))
                    sp.dma_start(KR[:, s3], keys[bass.ds(T.tile(3), 1)] if T.loop else keys[T.b + 3]
                                 ).then_inc(kr_in[s3], 16)
                if T.has(-1):
                    max_load(T, -1, 1)
                if T.has(-2):
                    s = T.slot(-2)
                    hold(sp, SP_H, o_copied, T.count(-2, J, J))
                    sp.dma_start(o_scr[s].rearrange("(j p) d -> p j d", p=P), O4[:, s]).then_inc(o_out[s], 16)
                if ahead(T):
                    s1 = T.slot(1)
                    hold(sp, SP_H, pv_done, T.count(-1, J, 0))
                    sp.dma_start(V[:, s1], vals[bass.ds(T.tile(1), 1)] if T.loop else vals[T.b + 1]
                                 ).then_inc(v_in[s1], 16)
                    part_write(T, 2, k_scr, KS, k_out, k_low, 1)
                if T.has(-2):
                    hold(sp, SP_H, o_out[s], T.slot_count(-2, 16))
                    sp.dma_start(SM[:, s, :], bass.AP(o_scr.tensor, (s * J * P + HR) * D,
                                                      [[32 * D, HPT], [1, D]])).then_inc(s_in[s], 16)
                    rows = o_scr[s].rearrange("(n r) d -> r n d", r=32)
                    hold(sp, SP_H, om_done, T.count(-4, 1, 0))
                    sp.dma_start(OC[:, s, :], rows[0:HR]).then_inc(o_in[s], 16)
                if T.has(0):
                    max_load(T, 0, 0)
                if ahead(T):
                    part_write(T, 2, q_scr, QS, q_out, ln1, 4)
                if T.has(-2):
                    hold(sp, SP_H, inverted, T.count(-2, 1, 1))
                    sp.dma_start(r_scr[s].rearrange("n d -> (n d)").rearrange("(p f) -> p f", p=P), SM[:, s, :]
                                 ).then_inc(r_out[s], 16)
                    hold(sp, SP_H, r_out[s], T.slot_count(-2, 16))
                    sp.dma_start(DN[:, s, :], bass.AP(r_scr.tensor, s * HPT * D, [[0, HR], [D, HPT], [1, D]])
                                 ).then_inc(r_in[s], 16)

            turns(sp, turn)
            for n in range(PW):
                sp.wait_ge(kr_in[n], 16 * len(range(n, TILES + 3, PW)))
                sp.wait_ge(k_in[n], 48 * len(range(n, TILES + 1, PW)))
                sp.wait_ge(q_in[n], 32 * len(range(n, TILES + 1, PW)))
                sp.wait_ge(v_in[n], 16 * len(range(n, TILES + 1, PW)))
                sp.wait_ge(k_out[n], 16 * len(range(n, TILES + 2, PW)))
                sp.wait_ge(q_out[n], 16 * len(range(n, TILES + 2, PW)))

            for n in range(PW):
                sp.wait_ge(dispatched[n], 16 * K8 * len(range(n, TILES, PW)))
            sp.wait_ge(tab_dve, TAB_OPS)
            over = sp.value_load(TAB[0:1, TAB_N - 1:TAB_N], min_val=0, max_val=NO)

            def load_expert(i, n):
                e = i * SLOTS + n
                if not isinstance(i, int):
                    for j in range(NJ):
                        hold(sp, SP_H, added[j], (e - SLOTS + 1) * 16)
                sp.dma_start(XE[:, n, 0:2, :].rearrange("p j c -> p (j c)"),
                             x_rows[bass.ds(e * CAP, 2 * P), :].rearrange("(p j) c -> p (j c)", j=2)
                             ).then_inc(xe_in[n], 16)
                sp.dma_start(XE[0:ROWS_J[2], n, 2, :], x_rows[bass.ds(e * CAP + 2 * P, ROWS_J[2]), :]
                             ).then_inc(xe_in[n], 16)
                sp.dma_start(W[:, n, :], wexp[bass.ds(e, 1)].rearrange("a p c -> (a p) c")).then_inc(w_in[n], 16)

            for n in range(SLOTS):
                load_expert(0, n)
            with sp.Fori(1, E // SLOTS) as i:
                for n in range(SLOTS):
                    load_expert(i, n)

            for j in range(NJ):
                sp.wait_ge(added[j], 16 * E)
            with sp.If(over > 0):
                with sp.Fori(0, E) as e:
                    r = sp.value_load(TAB[0:1, bass.ds(e + 2 * NO, 1)], min_val=0, max_val=DUMMY - P)
                    sp.dma_start(x_rows[bass.ds(r, P), :], FILL[:, 0, :]).then_inc(o_fill, 16)
                sp.wait_ge(o_fill, 16 * E)
                with sp.Fori(0, NO) as i:
                    r = sp.value_load(TAB[0:1, bass.ds(i, 1)], min_val=0, max_val=DUMMY)
                    e = sp.value_load(TAB[0:1, bass.ds(i + NO, 1)], min_val=0, max_val=E - 1)
                    hold(sp, SP_H, o_free, i + 1)
                    sp.dma_start(XE[:, 0, 0, :], x_rows[bass.ds(r, P), :]).then_inc(o_loaded, 16)
                    sp.dma_start(W[:, 0, :], wexp[bass.ds(e, 1)].rearrange("a p c -> (a p) c")
                                 ).then_inc(o_loaded, 16)
                sp.wait_ge(o_added, 16 * NO)

            def load_sums(i, n):
                t = i * FS + n
                if not isinstance(i, int):
                    hold(sp, SP_H, summed, (t - FS + 1) * 3)
                for j in range(NJ):
                    sp.dma_start(ACC[:, n, j, :], sums_dram[j][bass.ds(t * P, P), :]).then_inc(acc_in[n], 16)

            for n in range(FS):
                load_sums(0, n)
            with sp.Fori(1, TILES // FS) as i:
                for n in range(FS):
                    load_sums(i, n)
            for n in range(FS):
                sp.wait_ge(stored[n], 16 * TILES // FS)

        @block.gpsimd
        def _(pool):
            nc.gpsimd.memset(IDENT[:, :], 0.0).then_inc(pool_const, 1)
            nc.gpsimd.memset(UPPER[:, :], 1.0).then_inc(pool_const, 1)
            nc.gpsimd.memset(ONES[:, :], 1.0).then_inc(pool_const, 1)
            nc.gpsimd.memset(NHALF[:, :], -0.5).then_inc(pool_const, 1)
            nc.gpsimd.iota(IOTI[:, :], pattern=[[CAP, E]], base=1, channel_multiplier=0).then_inc(pool_const, 1)
            nc.gpsimd.memset(FILL[:, :, :], 0.0).then_inc(pool_const, 1)
            nc.gpsimd.iota(TOKEN[:, :], pattern=[[P, TILES]], base=0, channel_multiplier=1).then_inc(pool_const, 1)
            nc.gpsimd.iota(NI_I[:, :], pattern=[[1, NO]], base=0, channel_multiplier=0).then_inc(pool_const, 1)
            nc.gpsimd.iota(EI_I[:, 0:1], pattern=[[1, 1]], base=0, channel_multiplier=1).then_inc(pool_const, 1)
            nc.gpsimd.iota(EI_I[:, 1:2], pattern=[[1, 1]], base=0, channel_multiplier=CAP).then_inc(pool_const, 1)
            pool.wait_ge(pool_const, 10)
            for n in range(2):
                nc.gpsimd.iota(FILL[:, n, ROW - 1:ROW].bitcast(I32), pattern=[[1, 1]], base=TOK,
                               channel_multiplier=1).then_inc(pool_const, 1)
            nc.gpsimd.affine_select(out=IDENT[:, :], in_=IDENT[:, :], compare_op=ALU.not_equal, fill=1.0, base=0,
                                    pattern=[[-1, P]], channel_multiplier=1).then_inc(pool_const, 1)
            nc.gpsimd.affine_select(out=UPPER[:, :], in_=UPPER[:, :], compare_op=ALU.is_gt, fill=0.0, base=0,
                                    pattern=[[1, P]], channel_multiplier=-1).then_inc(pool_const, 1)
            pool.wait_ge(pool_const, 14)

            def fill(n):
                if n < 2 * E // 8:
                    c, n = divmod(n, E // 8)
                    return pool.dma_start(
                        bass.AP(x_rows.tensor, (8 * n * CAP + c * P) * ROW, [[2 * ROW, P // 2], [CAP * ROW, 8], [1, 2 * ROW]]),
                        bass.AP(FILL[:, :, :].tensor, c * (P // 2) * 2 * ROW, [[2 * ROW, P // 2], [0, 8], [1, 2 * ROW]])
                        ).then_inc(filled[c], 16)
                n -= 2 * E // 8
                if n < E // 16:
                    return pool.dma_start(
                        bass.AP(x_rows.tensor, (16 * n * CAP + 2 * P) * ROW,
                                [[ROW, ROWS_J[2]], [CAP * ROW, 16], [1, ROW]]),
                        bass.AP(FILL[:, :, :].tensor, 0, [[2 * ROW, ROWS_J[2]], [0, 16], [1, ROW]])).then_inc(filled[2], 16)
                return pool.dma_start(x_rows[DUMMY:DUMMY + P, :], FILL[:, 0, :]).then_inc(filled[2], 16)

            def deviation(T, d, mv, rs, ready, at, per_tile, done):
                s = T.slot(d)
                need(pool, ready, T.count(d, per_tile, at))
                nc.gpsimd.tensor_tensor(rs[:, s, 0:1], mv[:, s, 1:2], NHALF[:, :], ALU.pow).then_inc(done, 1)
                hold(pool, POOL_H, done, T.count(d, 2, 1))
                nc.gpsimd.tensor_scalar(rs[:, s, 1:2], mv[:, s, 0:1], rs[:, s, 0:1], -1.0, ALU.mult, ALU.mult
                                        ).then_inc(done, 1)

            def key_low(T, d):
                s = T.slot(d)
                if T.has(d - PW):
                    need(pool, k_out[s], T.slot_count(d - PW, 16))
                need(pool, k_high, T.count(d, 1, 1))
                nc.gpsimd.tensor_tensor(KS[:, s, 1], KR[:, s], KS[:, s, 0].bitcast(F32), ALU.subtract
                                        ).then_inc(k_low, 1)

            def dispatch(T, a, b):
                if T.has(-5):
                    s = T.slot(-5)
                    if a == 0:
                        if T.b in (5, 6) and not T.loop:
                            pool.wait_ge(filled[T.b - 5], 16 * E // 8)
                        hold(pool, POOL_H, place, T.count(-5, 5, 5))
                    for k in range(a, b):
                        pool.indirect_dma_start(x_rows, bass.IndirectOffsetOnAxis(ap=IDX[:, s, k:k + 1], axis=0),
                                                XN2[:, s, :], None).then_inc(dispatched[s], 16)

            key_low(Turn(0, 0), 0)
            deviation(Turn(0, 0), 0, MV1, RS1, ln1, 3, 4, rstd1)
            key_low(Turn(0, 0), 1)
            deviation(Turn(0, 0), 1, MV1, RS1, ln1, 3, 4, rstd1)
            for n in range(1, PW):
                pool.wait_ge(k_zero, n)
                nc.gpsimd.memset(K[0:MAXR, n].bitcast(F32), 0.0).then_inc(k_zero, 1)

            def turn(T):
                if not T.loop and T.b < 7:
                    for n in range(3 * T.b, 3 * T.b + 3):
                        fill(n)
                if not T.loop and TILES <= T.b < TILES + NJ:
                    pool.dma_start(sums_dram[T.b - TILES].rearrange("(p a) d -> p a d", p=P),
                                   bass.AP(ZERO[:, :].tensor, 0, [[D, P], [0, (TOK + P) // P], [1, D]])
                                   ).then_inc(sums_zero, 16)
                if T.has(-3):
                    s = T.slot(-3)
                    need(pool, o_in[s], T.slot_count(-3, 16))
                    need(pool, r_in[s], T.slot_count(-3, 16))
                    nc.gpsimd.tensor_tensor(OM[:, s], OC[:, s], DN[:, s], ALU.mult).then_inc(om_done, 1)
                if ahead(T):
                    deviation(T, 2, MV1, RS1, ln1, 3, 4, rstd1)
                    key_low(T, 2)
                dispatch(T, 0, 3)
                if T.has(-3):
                    deviation(T, -3, MV2, RS2, att, 4, 4, rstd2)
                dispatch(T, 3, 8)
                if not T.loop and T.b == 6:
                    pool.wait_ge(filled[2], 16 * (E // 16 + 1))

            turns(pool, turn)

            pool.wait_ge(tab_dve, TAB_OPS)
            pool.wait_ge(sums_zero, 16 * NJ)
            over = pool.value_load(TAB[0:1, TAB_N - 1:TAB_N], min_val=0, max_val=NO)

            def add_expert(i, n):
                e = i * SLOTS + n
                for j in range(NJ):
                    if not (isinstance(i, int) and e == 0):
                        hold(pool, POOL_H, added[j], e * 16)
                    hold(pool, POOL_H, y_weighted, e * NJ + (j + 1))
                    m = ROWS_J[j]
                    pool.indirect_dma_start(
                        sums_dram[j], bass.IndirectOffsetOnAxis(ap=XE[0:m, n, j, ROW - 1:ROW].bitcast(I32), axis=0),
                        Y[0:m, n % 2, j, :], None, compute_op=ALU.add).then_inc(added[j], 16)

            for n in range(SLOTS):
                add_expert(0, n)
            with pool.Fori(1, E // SLOTS) as i:
                for n in range(SLOTS):
                    add_expert(i, n)
            with pool.If(over > 0):
                pool.sem_inc(o_free, 1)
                with pool.Fori(0, NO) as i:
                    hold(pool, POOL_H, o_weighted, i + 1)
                    pool.indirect_dma_start(
                        sums_dram[0], bass.IndirectOffsetOnAxis(ap=XE[:, 0, 0, ROW - 1:ROW].bitcast(I32), axis=0),
                        Y[:, 0, 0, :], None, compute_op=ALU.add).then_inc(o_added, 16)
                    hold(pool, POOL_H, o_added, i * 16 + 16)
                    pool.sem_inc(o_free, 1)

        @block.vector
        def _(dve):
            nc.vector.memset(ZERO[:, :], 0.0).then_inc(dve_const, 1)
            nc.vector.memset(Q[0:MAXR, 0].bitcast(F32), 0.0).then_inc(q_zero, 1)
            nc.vector.memset(X[:, TILES:TILES + 2, :], 0.0).then_inc(dve_const, 1)
            nc.vector.memset(SEEN[:, 0, :], 0.0).then_inc(dve_const, 1)
            nc.vector.memset(ONESF[:, :], 1.0).then_inc(dve_const, 1)
            dve.wait_ge(pool_const, 10)
            nc.vector.tensor_copy(BASE1[:, :], IOTI[:, :]).then_inc(dve_const, 1)
            nc.vector.tensor_copy(NI[:, :], NI_I[:, :]).then_inc(dve_const, 1)
            nc.vector.tensor_copy(EI[:, :], EI_I[:, :]).then_inc(dve_const, 1)
            dve.wait_ge(dve_const, 7)

            def ln1_stats(T, d):
                s, at = T.slot(d), T.tile(d)
                xs = X[:, bass.ds(at, 1), :].rearrange("p a d -> p (a d)") if T.loop else X[:, at, :]
                nc.vector.bn_stats(ST1[:, s], xs).then_inc(ln1, 1)
                need(dve, ln1, T.count(d, 4, 1))
                nc.vector.bn_aggr(MV1[:, s], ST1[:, s]).then_inc(ln1, 1) if not T.loop else aggr(MV1[:, s], ST1[:, s], ln1)
                need(dve, ln1, T.count(d, 4, 2))
                nc.vector.tensor_scalar(MV1[:, s, 1:2], MV1[:, s, 1:2], EPS, None, ALU.add).then_inc(ln1, 1)

            def aggr(o, a, s):
                dve.sem_inc(DVE_H, 1)
                nc.vector.bn_aggr(o, a).then_inc(s, 1)

            def q_low(T, d):
                s = T.slot(d)
                if T.has(d - PW):
                    need(dve, q_out[s], T.slot_count(d - PW, 16))
                need(dve, norm1, T.count(d, 2, 2))
                nc.vector.tensor_tensor(QS[:, s, 1], XN[:, s], QS[:, s, 0].bitcast(F32), ALU.subtract
                                        ).then_inc(ln1, 1)

            def take_max(T, u):
                h = u // 4
                pair = POS[f"u{u}"] % 2
                if u % 4 == 0:
                    need(dve, misc_b if h == 0 else misc_a, T.count(0, 1, 0) if h == 0 else T.count(0, 1, 0))
                need(dve, scored, T.count(0, UNITS, u + 1))
                nc.vector.tensor_reduce(MX[:, h, 4 * (u % 4):4 * (u % 4) + 4],
                                        SC[:, pair, :, :].rearrange("p a (m n) -> p (a m) n", m=MT),
                                        axis=AX_X, op=ALU.max, negate=True).then_inc(max_done, 1)

            def max_low(T, d, h, pair):
                need(dve, mxt_high, T.count(d, 2, h + 1))
                nc.vector.tensor_tensor(MXT[:, h, 1, :], SC[0:16, pair, 0, 0:P], MXT[:, h, 0, :].bitcast(F32),
                                        ALU.subtract).then_inc(mxt_low, 1)

            def ma(T):
                pair = POS["MA"] % 2
                if T.has(-1):
                    max_low(T, -1, 1, pair)
                if T.has(-5):
                    need(dve, misc_a, T.count(0, 1, 0))
                    s = T.slot(-5)
                    nc.vector.tensor_tensor(SL[:, s], SC[:, pair, 0, P:P + E], BASE1[:, :], ALU.add).then_inc(place, 1)

            def mb(T):
                pair = POS["MB"] % 2
                if T.has(0):
                    max_low(T, 0, 0, pair)
                if T.has(-4):
                    need(dve, misc_b, T.count(0, 1, 1))
                    s = T.slot(-4)
                    nc.vector.tensor_reduce(NM[:, s], SC[:, pair, 1, 0:E], axis=AX_X, op=ALU.max,
                                            negate=True).then_inc(route, 1)

            def place_rest(T):
                s, at = T.slot(-5), T.tile(-5)
                need(dve, place, T.count(-5, 5, 1))
                nc.vector.tensor_tensor(SLM[:, s], SL[:, s], MASK[:, s], ALU.mult).then_inc(place, 1)
                hold(dve, DVE_H, place, T.count(-5, 5, 2))
                nc.vector.max(S8[:, s], SLM[:, s]).then_inc(place, 1)
                need(dve, place, T.count(-5, 5, 3))
                nc.vector.tensor_scalar(IDX[:, s], S8[:, s], -1.0, None, ALU.add).then_inc(place, 1)
                a = bass.ds(at, 1) if T.loop else slice(at, at + 1)
                nc.vector.tensor_copy(XN2[:, s, ROW - 1:ROW].bitcast(I32), TOKEN[:, a]).then_inc(place, 1)

            def route_rest(T):
                s = T.slot(-4)
                need(dve, rexp, T.count(-4, 1, 1))
                nc.vector.reciprocal(RSE[:, s], SE[:, s]).then_inc(route, 1)
                need(dve, route, T.count(-4, 8, 2))
                nc.vector.tensor_scalar(PR[:, s], EX[:, s], RSE[:, s], None, ALU.mult).then_inc(route, 1)
                hold(dve, DVE_H, route, T.count(-4, 8, 3))
                nc.vector.max(TOP[:, s], PR[:, s]).then_inc(route, 1)
                hold(dve, DVE_H, route, T.count(-4, 8, 4))
                nc.vector.match_replace(REST[:, s], TOP[:, s], PR[:, s], -1.0).then_inc(route, 1)
                need(dve, route, T.count(-4, 8, 5))
                nc.vector.tensor_scalar(MASK[:, s], REST[:, s], 0.0, None, ALU.is_lt).then_inc(route, 1)
                need(dve, route, T.count(-4, 8, 6))
                nc.vector.tensor_tensor(XN2[:, s, D:D + E], PR[:, s], MASK[:, s], ALU.mult).then_inc(route, 1)
                nc.vector.tensor_tensor(SEEN[:, T.slot(-3)], SEEN[:, s], MASK[:, s], ALU.add).then_inc(route, 1)

            def x_at(T, d):
                at = T.tile(d)
                return X[:, bass.ds(at, 1), :].rearrange("p a d -> p (a d)") if T.loop else X[:, at, :]

            def invert(T):
                s = T.slot(-2)
                need(dve, s_in[s], T.slot_count(-2, 16))
                nc.vector.reciprocal(SM[:, s], SM[:, s]).then_inc(inverted, 1)

            def residual(T):
                s = T.slot(-3)
                need(dve, om_done, T.count(-3, 1, 1))
                nc.vector.scalar_tensor_tensor(out=x_at(T, -3), in0=OM[:, s], scalar=TG[:, 0:1], in1=x_at(T, -3),
                                               op0=ALU.mult, op1=ALU.add).then_inc(att, 1)
                hold(dve, DVE_H, att, T.count(-3, 4, 1))
                nc.vector.bn_stats(ST2[:, s], x_at(T, -3)).then_inc(att, 1)
                hold(dve, DVE_H, att, T.count(-3, 4, 2))
                nc.vector.bn_aggr(MV2[:, s], ST2[:, s]).then_inc(att, 1)
                need(dve, att, T.count(-3, 4, 3))
                nc.vector.tensor_scalar(MV2[:, s, 1:2], MV2[:, s, 1:2], EPS, None, ALU.add).then_inc(att, 1)

            dve.wait_ge(x_in, 16)
            for n in range(2):
                ln1_stats(Turn(0, 0), n)
                q_low(Turn(0, 0), n)
            nc.vector.memset(Q[0:MAXR, 1].bitcast(F32), 0.0).then_inc(q_zero, 1)
            dve.wait_ge(tanh_done, 1)

            def turn(T):
                if T.has(0):
                    take_max(T, 0)
                ma(T)
                if T.has(0):
                    take_max(T, 1)
                if ahead(T):
                    if not T.loop and T.b == 0:
                        dve.wait_ge(x_in, 32)
                    ln1_stats(T, 2)
                if T.has(-5):
                    place_rest(T)
                if T.has(0):
                    take_max(T, 2)
                    take_max(T, 3)
                if T.has(-3):
                    residual(T)
                if T.has(0):
                    take_max(T, 4)
                mb(T)
                if T.has(0):
                    take_max(T, 5)
                if ahead(T):
                    q_low(T, 2)
                if T.has(-2):
                    invert(T)
                if T.has(0):
                    take_max(T, 6)
                if T.has(-4):
                    route_rest(T)
                if T.has(0):
                    take_max(T, 7)
                if not T.loop and T.b == 0:
                    nc.vector.memset(Q[0:MAXR, 2].bitcast(F32), 0.0).then_inc(q_zero, 1)

            turns(dve, turn)

            n_tab = [0]

            def tab(ins, last=False):
                n_tab[0] += 1
                ins.then_inc(tab_dve, 1)
                if not last:
                    dve.wait_ge(tab_dve, n_tab[0])

            dve.wait_ge(tab_pe, 1)
            tab(nc.vector.tensor_copy(CNT[:, 0:1], SC[0:E, 0, 0, 0:1]))
            tab(nc.vector.tensor_scalar(CNT[:, 7:8], CNT[:, 0:1], float(MAIN), None, ALU.max))
            tab(nc.vector.tensor_scalar(CNI[:, 0:1], CNT[:, 7:8], float(P - 1 - MAIN), None, ALU.add))
            tab(nc.vector.tensor_scalar(CNI[:, 1:2], CNI[:, 0:1], 7, None, ALU.arith_shift_right))
            tab(nc.vector.tensor_copy(CNT[:, 1:2], CNI[:, 1:2]))
            tab(nc.vector.tensor_copy(NTB[:, :], CNI[:, 1:2]))
            dve.wait_ge(tab_pe, 2)
            tab(nc.vector.tensor_copy(CNT[:, 2:3], SC[0:E, 0, 1, 0:1]))
            tab(nc.vector.tensor_tensor(CNT[:, 3:4], CNT[:, 2:3], CNT[:, 1:2], ALU.add))
            tab(nc.vector.tensor_scalar(A1[:, :], NI[:, :], CNT[:, 2:3], None, ALU.is_ge))
            tab(nc.vector.tensor_scalar(A2[:, :], NI[:, :], CNT[:, 3:4], None, ALU.is_lt))
            tab(nc.vector.tensor_tensor(A1[:, :], A1[:, :], A2[:, :], ALU.mult))
            tab(nc.vector.tensor_scalar(RB[:, :], NI[:, :], CNT[:, 2:3], float(P), ALU.subtract, ALU.mult))
            tab(nc.vector.tensor_scalar(RB[:, :], RB[:, :], EI[:, 1:2], float(MAIN - DUMMY), ALU.add, ALU.add))
            tab(nc.vector.tensor_tensor(TB[:, 0:NO], RB[:, :], A1[:, :], ALU.mult))
            tab(nc.vector.tensor_scalar(TB[:, NO:2 * NO], A1[:, :], EI[:, 0:1], None, ALU.mult))
            tab(nc.vector.tensor_tensor(CNT[:, 4:5], CNT[:, 7:8], EI[:, 1:2], ALU.add))
            tab(nc.vector.tensor_scalar(TB[:, 2 * NO:2 * NO + E], IDENT[0:E, 0:E], CNT[:, 4:5], None, ALU.mult))
            tab(nc.vector.tensor_copy(TB[:, 2 * NO + E:TAB_N], CNT[:, 1:2]))
            dve.wait_ge(tab_pe, 3)
            tab(nc.vector.tensor_copy(TABF[:, :], SC[0:1, 1, 0, 0:TAB_N]))
            tab(nc.vector.tensor_scalar(TABF[:, 0:NO], TABF[:, 0:NO], float(DUMMY), None, ALU.add))
            tab(nc.vector.tensor_copy(TAB[:, :], TABF[:, :]))
            assert n_tab[0] == TAB_OPS
            over = dve.value_load(TAB[0:1, TAB_N - 1:TAB_N], min_val=0, max_val=NO)

            def hidden(i, n):
                e, b = i * SLOTS + n, n % 2
                need(dve, silu_done, e + 1)
                if not (isinstance(i, int) and e < 2):
                    need(dve, y_ps, e - 1)
                nc.vector.tensor_tensor(HT[:, b, :], GU[:, b, 1, :], SG[:, b, :], ALU.mult).then_inc(h_done, 1)

            def weighted(i, n):
                e, b = i * SLOTS + n, n % 2
                need(dve, y_ps, e + 1)
                for j in range(NJ):
                    if not (isinstance(i, int) and e < 2):
                        need(dve, added[j], (e - 1) * 16)
                    m = ROWS_J[j]
                    nc.vector.tensor_scalar(Y[0:m, b, j, :], YP[j][0:m], XE[0:m, n % SLOTS, j, bass.ds(e + D, 1)],
                                            None, ALU.mult).then_inc(y_weighted, 1)

            for n in range(SLOTS):
                hidden(0, n)
                if n:
                    weighted(0, n - 1)
            with dve.Fori(1, E // SLOTS) as i:
                for n in range(SLOTS):
                    hidden(i, n)
                    weighted(i, n - 1)
            weighted(E // SLOTS - 1, SLOTS - 1)

            with dve.If(over > 0):
                with dve.Fori(0, NO) as i:
                    need(dve, o_silu, i + 1)
                    nc.vector.tensor_tensor(HT[:, 0, 0:P], GU[:, 0, 1, 0:P], SG[:, 0, 0:P], ALU.mult).then_inc(o_h, 1)
                    need(dve, o_y_ps, i + 1)
                    e = dve.value_load(TAB[0:1, bass.ds(i + NO, 1)], min_val=0, max_val=E - 1)
                    nc.vector.tensor_scalar(Y[:, 0, 0, :], YP[0], XE[:, 0, 0, bass.ds(e + D, 1)], None, ALU.mult
                                            ).then_inc(o_weighted, 1)

            def final(i, n):
                t = i * FS + n
                a = bass.ds(t, 1) if not isinstance(i, int) else slice(t, t + 1)
                need(dve, acc_in[n], i * (16 * NJ) + 16 * NJ)
                nc.vector.tensor_tensor(ACC[:, n, 0, :], ACC[:, n, 0, :], ACC[:, n, 1, :], ALU.add).then_inc(summed, 1)
                need(dve, summed, t * 3 + 1)
                nc.vector.tensor_tensor(ACC[:, n, 0, :], ACC[:, n, 0, :], ACC[:, n, 2, :], ALU.add).then_inc(summed, 1)
                if not isinstance(i, int):
                    need(dve, stored[n], i * 16)
                hold(dve, DVE_H, summed, t * 3 + 2)
                nc.vector.scalar_tensor_tensor(out=OT[:, n:n + 1, :], in0=ACC[:, n, 0:1, :], scalar=TG[:, 1:2],
                                               in1=X[:, a, :], op0=ALU.mult, op1=ALU.add).then_inc(summed, 1)

            for n in range(FS):
                final(0, n)
            with dve.Fori(1, TILES // FS) as i:
                for n in range(FS):
                    final(i, n)

        @block.scalar
        def _(act):
            act.wait_ge(gates_in, 32)
            nc.scalar.activation(TG[:, :], GIN[:, :], ACT.Tanh).then_inc(tanh_done, 1)

            def x_at(T, d):
                at = T.tile(d)
                return X[:, bass.ds(at, 1), :].rearrange("p a d -> p (a d)") if T.loop else X[:, at, :]

            def key_high(T, d):
                s = T.slot(d)
                if T.has(d - PW):
                    need(act, k_out[s], T.slot_count(d - PW, 16))
                need(act, kr_in[s], T.slot_count(d, 16))
                nc.scalar.copy(KS[:, s, 0], KR[:, s]).then_inc(k_high, 1)

            def normalise1(T, d):
                s = T.slot(d)
                hold(act, ACT_H, ln1, T.count(d - 2, 4, 0))
                hold(act, ACT_H, rstd1, T.count(d, 2, 2))
                nc.scalar.activation(XN[:, s], x_at(T, d), ACT.Identity, scale=RS1[:, s, 0:1], bias=RS1[:, s, 1:2]
                                     ).then_inc(norm1, 1)
                if T.has(d - PW):
                    need(act, q_out[s], T.slot_count(d - PW, 16))
                need(act, norm1, T.count(d, 2, 1))
                nc.scalar.copy(QS[:, s, 0], XN[:, s]).then_inc(norm1, 1)

            def normalise2(T):
                s = T.slot(-3)
                if T.has(-6):
                    hold(act, ACT_H, dispatched[s], T.slot_count(-6, 16 * K8))
                hold(act, ACT_H, rstd2, T.count(-3, 2, 2))
                nc.scalar.activation(XN2[:, s, 0:D], x_at(T, -3), ACT.Identity, scale=RS2[:, s, 0:1], bias=RS2[:, s, 1:2]
                                     ).then_inc(norm2, 1)

            def max_high(T, d, h, name):
                need(act, max_in[h], T.count(d, 32, 0))
                need(act, misc_a if h else misc_b, T.count(0, 1, 0 if h else 1))
                nc.scalar.copy(MXT[:, h, 0, :], SC[0:16, POS[name] % 2, 0, 0:P]).then_inc(mxt_high, 1)

            act.wait_ge(dve_const, 1)
            nc.scalar.copy(K[0:MAXR, 0].rearrange("p n d -> p (n d)"),
                           bass.AP(ZERO[:, :].tensor, 0, [[D, MAXR], [0, HPT], [1, D]])).then_inc(k_zero, 1)
            for n in range(2):
                key_high(Turn(0, 0), n)
            for n in range(2):
                normalise1(Turn(0, 0), n)

            def turn(T):
                for u in range(UNITS):
                    if T.has(-1):
                        for a in range(2):
                            n = 2 * u + a
                            h = HPT * (T.b - 1) + n
                            if n % 4 == 0:
                                need(act, pv_done, T.count(-1, J, n // 4 - EXP_RING // 4 + 1))
                            need(act, st_done, T.count(-1, HPT, n + 1))
                            nc.scalar.activation(PE_T[:, h % EXP_RING, :], ST[:, h % 3, :], ACT.Exp,
                                                 scale=SCALE).then_inc(exp_done, 1)
                    if u == 0:
                        if T.has(-1):
                            max_high(T, -1, 1, "MA")
                        if T.has(-4):
                            s = T.slot(-4)
                            need(act, misc_a, T.count(0, 1, 0))
                            nc.scalar.copy(XT2[:, s], SC[:, POS["MA"] % 2, 1, 0:D]).then_inc(xt_copied, 1)
                    if u == 1 and ahead(T):
                        key_high(T, 2)
                    if u == 3 and ahead(T):
                        normalise1(T, 2)
                    if u == 4 and T.has(0):
                        max_high(T, 0, 0, "MB")
                    if u == 5 and T.has(-4):
                        s = T.slot(-4)
                        need(act, route, T.count(-4, 8, 1))
                        nc.scalar.activation(EX[:, s], SC[:, POS["MB"] % 2, 1, 0:E], ACT.Exp, bias=NM[:, s],
                                             accum_out=SE[:, s]).then_inc(rexp, 1)
                    if u == 6 and T.has(-3):
                        normalise2(T)
                    if u % 2 == 0:
                        d, j = (-2, 2 + u // 2) if u < 4 else (-1, (u - 4) // 2)
                        if T.has(d):
                            s = T.slot(d)
                            if j == 0:
                                if T.loop or T.b + d - PW >= 0:
                                    need(act, o_out[s], T.slot_count(d - PW, 16))
                            need(act, pv_done, T.count(d, J, j + 1))
                            nc.scalar.copy(O4[:, s, j, :], OX[:, 0:D]).then_inc(o_copied, 1)

            turns(act, turn)

            act.wait_ge(tab_dve, TAB_OPS)
            over = act.value_load(TAB[0:1, TAB_N - 1:TAB_N], min_val=0, max_val=NO)

            def rows_copy(i, n):
                e, b = i * SLOTS + n, n % 2
                need(act, xt_ps, e + 1)
                if not (isinstance(i, int) and e < 2):
                    need(act, gu_ps, e - 1)
                nc.scalar.copy(XET[:, b], XP).then_inc(xet, 1)

            def gate(i, n):
                e, b = i * SLOTS + n, n % 2
                if not (isinstance(i, int) and e < 2):
                    need(act, h_done, e - 1)
                need(act, gu_ps, e + 1)
                nc.scalar.activation(SG[:, b, :], GU[:, b, 0, :], ACT.Silu).then_inc(silu_done, 1)

            rows_copy(0, 0)
            for n in range(SLOTS):
                rows_copy(0, n + 1)
                gate(0, n)
            with act.Fori(1, E // SLOTS - 1) as i:
                for n in range(SLOTS):
                    rows_copy(i, n + 1)
                    gate(i, n)
            for n in range(SLOTS):
                if n + 1 < SLOTS:
                    rows_copy(E // SLOTS - 1, n + 1)
                gate(E // SLOTS - 1, n)

            with act.If(over > 0):
                with act.Fori(0, NO) as i:
                    need(act, o_xt_ps, i + 1)
                    nc.scalar.copy(XET[:, 0, :, 0:P], XP[:, :, 0:P]).then_inc(o_xet, 1)
                    need(act, o_gu_ps, i + 1)
                    nc.scalar.activation(SG[:, 0, 0:P], GU[:, 0, 0, 0:P], ACT.Silu).then_inc(o_silu, 1)

            def store(i, n):
                t = i * FS + n
                hold(act, ACT_H, summed, t * 3 + 3)
                act.dma_start(out[bass.ds(t * P, P), :], OT[:, n, :]).then_inc(stored[n], 16)

            with act.Fori(0, TILES // FS) as i:
                for n in range(FS):
                    store(i, n)

        @block.tensor
        def _(pe):
            pe.wait_ge(pool_const, 14)
            pe.wait_ge(dve_const, 7)

            def slot_free(T, name):
                at = POS[name] - 2
                d = 0
                if at < 0:
                    at, d = at + len(NAMES), -1
                before = NAMES[at]
                if before == "MA":
                    if T.has(d - 1):
                        need(pe, mxt_low, T.count(d - 1, 2, 2))
                    if T.has(d - 4):
                        need(pe, xt_copied, T.count(d - 4, 1, 1))
                    if T.has(d - 5):
                        need(pe, place, T.count(d - 5, 5, 1))
                elif before == "MB":
                    if T.has(d):
                        need(pe, mxt_low, T.count(d, 2, 1))
                    if T.has(d - 4):
                        need(pe, rexp, T.count(d - 4, 1, 1))
                elif T.has(d):
                    need(pe, max_done, T.count(d, UNITS, int(before[1]) + 1))

            def step(T, u):
                s0, s1 = T.slot(0), T.slot(-1)
                if T.has(0):
                    if u == 0:
                        if not T.loop and T.b < PW:
                            pe.wait_ge(k_ones, 16)
                        need(pe, k_in[s0], T.slot_count(0, 48))
                        need(pe, q_in[s0], T.slot_count(0, 32))
                    slot_free(T, f"u{u}")
                pair = POS[f"u{u}"] % 2
                if T.has(0):
                    for a in range(2):
                        n = 2 * u + a
                        for r in range(MT):
                            mm = nc.tensor.matmul(SC[:, pair, a, r * D:(r + 1) * D],
                                                  Q[0:MAXR, s0, n, r * P:(r + 1) * P], K[0:MAXR, s0, n, :],
                                                  start=True, stop=True)
                    mm.then_inc(scored, 1)
                if T.has(-1):
                    if u % 4 == 0:
                        need(pe, max_in[u // 4], T.count(-1, 32, 32))
                    for a in range(2):
                        n = 2 * u + a
                        bank = (HPT * (T.b - 1) + n) % 3
                        need(pe, exp_done, T.count(-1, HPT, n - 2))
                        for r in range(MT):
                            mm = nc.tensor.matmul(ST[:, bank, r * D:(r + 1) * D],
                                                  K[:, s1, n, r * P:(r + 1) * P], Q[:, s1, n, :],
                                                  start=True, stop=True)
                        mm.then_inc(st_done, 1)

            def sums(T, d, j):
                s = T.slot(d)
                if j == 0:
                    need(pe, v_in[s], T.slot_count(d, 16))
                need(pe, exp_done, T.count(d, HPT, 4 * j + 4))
                need(pe, o_copied, T.count(d, J, j))
                for r in range(MT):
                    for g in range(G):
                        h = HPT * (T.b + d) + 4 * j + g
                        c = (4 * j + g) * VC
                        mm = nc.tensor.matmul(OX[32 * g:32 * g + 32, 0:D], V[:, s, r, c:c + 32],
                                              PE_T[:, h % EXP_RING, r * D:(r + 1) * D],
                                              start=(r == 0), stop=(r == 1))
                mm.then_inc(pv_done, 1)

            def ma(T):
                if not (T.has(-1) or T.has(-4) or T.has(-5)):
                    return
                slot_free(T, "MA")
                pair = POS["MA"] % 2
                if T.has(-1):
                    need(pe, max_done, T.count(-1, UNITS, UNITS))
                    mm = nc.tensor.transpose(SC[0:16, pair, 0, 0:P], MX[:, 1, :], IDENT[:, :])
                if T.has(-5):
                    s = T.slot(-5)
                    need(pe, route, T.count(-5, 8, 8))
                    nc.tensor.matmul(SC[:, pair, 0, P:P + E], UPPER[:, :], MASK[:, s], start=True, stop=False)
                    mm = nc.tensor.matmul(SC[:, pair, 0, P:P + E], ONES[:, :], SEEN[:, s], start=False, stop=True)
                if T.has(-4):
                    s = T.slot(-4)
                    need(pe, norm2, T.count(-4, 1, 1))
                    for k in range(MT):
                        mm = nc.tensor.transpose(SC[:, pair, 1, k * P:(k + 1) * P], XN2[:, s, k * P:(k + 1) * P],
                                                 IDENT[:, :])
                mm.then_inc(misc_a, 1)

            def mb(T):
                if not (T.has(0) or T.has(-4)):
                    return
                slot_free(T, "MB")
                pair = POS["MB"] % 2
                if T.has(0):
                    need(pe, max_done, T.count(0, UNITS, 4))
                    mm = nc.tensor.transpose(SC[0:16, pair, 0, 0:P], MX[:, 0, :], IDENT[:, :])
                if T.has(-4):
                    s = T.slot(-4)
                    if not T.loop and T.b == 4:
                        pe.wait_ge(router_in, 16)
                    need(pe, xt_copied, T.count(-4, 1, 1))
                    for k in range(MT):
                        mm = nc.tensor.matmul(SC[:, pair, 1, 0:E], XT2[:, s, k * P:(k + 1) * P], RW[:, k, :],
                                              start=(k == 0), stop=(k == MT - 1))
                mm.then_inc(misc_b, 1)

            def turn(T):
                for u in range(UNITS):
                    step(T, u)
                    if u == 0:
                        ma(T)
                    if u == 4:
                        mb(T)
                    if u == 1 and T.has(-2):
                        sums(T, -2, 3)
                    if u in (3, 5, 7) and T.has(-1):
                        sums(T, -1, (u - 3) // 2)

            turns(pe, turn)

            last = TILES % PW
            pe.wait_ge(route, 8 * TILES)
            pe.wait_ge(place, 5 * TILES)
            nc.tensor.matmul(SC[0:E, 0, 0, 0:1], SEEN[:, last], ONES[:, 0:1], start=True, stop=True
                             ).then_inc(tab_pe, 1)
            pe.wait_ge(tab_dve, 6)
            nc.tensor.matmul(SC[0:E, 0, 1, 0:1], UPPER[0:E, 0:E], NTB[:, :], start=True, stop=True
                             ).then_inc(tab_pe, 1)
            pe.wait_ge(tab_dve, TAB_OPS - 3)
            nc.tensor.matmul(SC[0:1, 1, 0, 0:TAB_N], ONESF[:, 0:1], TB[:, :], start=True, stop=True
                             ).then_inc(tab_pe, 1)
            pe.wait_ge(tab_dve, TAB_OPS)
            over = pe.value_load(TAB[0:1, TAB_N - 1:TAB_N], min_val=0, max_val=NO)

            def rows_t(i, n):
                e, s = i * SLOTS + n, n % SLOTS
                need(pe, xe_in[s], (i + n // SLOTS) * 32 + 32)
                if not (isinstance(i, int) and e < 1):
                    need(pe, xet, e)
                for k in range(MT):
                    for j, m in enumerate(ROWS_J):
                        mm = nc.tensor.transpose(XP[:, k, j * P:j * P + m], XE[0:m, s, j, k * P:(k + 1) * P],
                                                 IDENT[0:m, 0:m])
                mm.then_inc(xt_ps, 1)

            def gate_up(i, n):
                e, b = i * SLOTS + n, n % 2
                need(pe, xet, e + 1)
                need(pe, w_in[n], i * 16 + 16)
                if not (isinstance(i, int) and e < 2):
                    need(pe, h_done, e - 1)
                for c in range(2):
                    for k in range(MT):
                        mm = nc.tensor.matmul(GU[:, b, c, :], W[:, n, k * 2 * I + c * I:k * 2 * I + (c + 1) * I],
                                              XET[:, b, k, :], start=(k == 0), stop=(k == MT - 1))
                mm.then_inc(gu_ps, 1)

            def down(i, n):
                e, b, s = i * SLOTS + n, n % 2, n % SLOTS
                need(pe, h_done, e + 1)
                if not (isinstance(i, int) and e < 1):
                    need(pe, y_weighted, e * NJ)
                for j, m in enumerate(ROWS_J):
                    mm = nc.tensor.matmul(YP[j][0:m], HT[:, b, j * P:j * P + m], W[:, s, 4 * I:], start=True, stop=True)
                mm.then_inc(y_ps, 1)

            rows_t(0, 0)
            for n in range(SLOTS):
                rows_t(0, n + 1)
                gate_up(0, n)
                if n:
                    down(0, n - 1)
            with pe.Fori(1, E // SLOTS - 1) as i:
                for n in range(SLOTS):
                    rows_t(i, n + 1)
                    gate_up(i, n)
                    down(i, n - 1)
            last = E // SLOTS - 1
            for n in range(SLOTS):
                if n + 1 < SLOTS:
                    rows_t(last, n + 1)
                gate_up(last, n)
                down(last, n - 1)
            down(last, SLOTS - 1)

            with pe.If(over > 0):
                with pe.Fori(0, NO) as i:
                    need(pe, o_loaded, i * 32 + 32)
                    for k in range(MT):
                        mm = nc.tensor.transpose(XP[:, k, 0:P], XE[:, 0, 0, k * P:(k + 1) * P], IDENT[:, :])
                    mm.then_inc(o_xt_ps, 1)
                    need(pe, o_xet, i + 1)
                    for c in range(2):
                        for k in range(MT):
                            mm = nc.tensor.matmul(GU[:, 0, c, 0:P], W[:, 0, k * 2 * I + c * I:k * 2 * I + (c + 1) * I],
                                                  XET[:, 0, k, 0:P], start=(k == 0), stop=(k == MT - 1))
                    mm.then_inc(o_gu_ps, 1)
                    need(pe, o_h, i + 1)
                    nc.tensor.matmul(YP[0], HT[:, 0, 0:P], W[:, 0, 4 * I:], start=True, stop=True).then_inc(o_y_ps, 1)


def kernel(x, ctx_2048, g_xattn, g_ffn, L0_ffn_router_weight, L0_ffn_gate_up_proj, L0_ffn_down_proj):
    import numpy as np
    import concourse.bacc as bacc
    from concourse.bass_utils import run_bass_kernel_spmd as run

    f = np.float32

    def tiles(a):
        return np.ascontiguousarray(a).reshape(TILES, HPT, HR, D).transpose(0, 2, 1, 3).reshape(TILES, P, D)

    rows = tiles(x).reshape(TOK, D)
    keys = np.zeros((TILES + 3, P, D), f)
    keys[:TILES] = tiles(ctx_2048)
    vals = np.ones((TILES + 1, P, MT, VW), f)
    ctx_t = np.ascontiguousarray(ctx_2048).reshape(TILES, HPT, HR, MT, P).transpose(0, 4, 3, 1, 2)
    heads = np.ones((TILES, P, MT, HPT, VC), f)
    heads[..., :HR] = ctx_t
    vals[:TILES, :, :, :HPT * VC] = heads.reshape(TILES, P, MT, HPT * VC)
    gu = np.ascontiguousarray(L0_ffn_gate_up_proj).reshape(E, 2 * I, MT, P).transpose(0, 3, 2, 1).reshape(E, P, 4 * I)
    dn = np.ascontiguousarray(L0_ffn_down_proj).transpose(0, 2, 1)
    arrays = {
        "x_in_dram": rows,
        "keys_dram": keys,
        "vals_dram": vals,
        "g_attn_dram": np.ascontiguousarray(g_xattn).reshape(1),
        "g_ffn_dram": np.ascontiguousarray(g_ffn).reshape(1),
        "router_dram": np.ascontiguousarray(np.asarray(L0_ffn_router_weight).T),
        "experts_dram": np.ascontiguousarray(np.concatenate([gu, dn], axis=2)),
    }
    nc = bacc.Bacc("TRN2", target_bir_lowering=False, num_devices=1)
    aps = [nc.dram_tensor(n, a.shape, F32, kind="ExternalInput").ap() for n, a in arrays.items()]
    out = nc.dram_tensor("out_dram", (TOK, D), F32, kind="ExternalOutput").ap()
    build(nc, *aps, out)
    r = run(nc, [arrays], core_ids=[0])
    got = r.results[0]["out_dram"].reshape(TILES, HR, HPT, D).transpose(0, 2, 1, 3)
    return np.ascontiguousarray(got).reshape(B, S, D)
```

```python
from contextlib import ExitStack

import concourse.bass as bass
from concourse import mybir

F32 = mybir.dt.float32
BF16 = mybir.dt.bfloat16
F32R = mybir.dt.float32r
I32 = mybir.dt.int32
ALU = mybir.AluOpType
ACT = mybir.ActivationFunctionType
AX_X = mybir.AxisListType.X

P = 128
D = 256
B, S = 32, 64
TOK = B * S
N_HEAD = 8
HR = S // N_HEAD
TILES = TOK // P
HPT = P // HR
G = 4
J = HPT // G
MT = D // P
SCALE = float(HR) ** -0.5
EPS = 1e-5
VC = HR + 1
VW = HPT * VC + 32 - VC
E = 64
I = 128
K8 = 8
CAP = TOK + P
MAIN = 320
ROWS_J = (P, P, MAIN - 2 * P)
NJ = len(ROWS_J)
NS = 4
ROW = D + E + 1
DUMMY = E * CAP
SLOTS = 8
WS = 4
PRODUCTS = ((0, 0), (0, 1), (1, 0))
FS = 8
NO = max(k * (min(TOK, TOK * K8 // k) - MAIN + P - 1) // P for k in range(1, E + 1) if TOK * K8 // k > MAIN)
WCOLS = 2 * 2 * I + D
EXP_RING = 12
PW = 3
TAB_OPS = 21
TAB_N = 2 * NO + E + 1
TURNS_FIRST = 7
PARTS = 2
MAXR = 96
LAST = 5
ZR = -(-(TOK + P) // (TILES - TURNS_FIRST) // P) * P


class Turn:

    def __init__(self, i, b):
        self.i, self.b = i, b
        self.loop = not isinstance(i, int)

    def tile(self, d):
        return self.i * PW + (self.b + d)

    def slot(self, d):
        return (self.b + d) % PW

    def count(self, d, per_tile, extra):
        return self.i * (PW * per_tile) + ((self.b + d) * per_tile + extra)

    def slot_count(self, d, per_use, extra=0):
        return self.i * per_use + (((self.b + d) // PW + 1) * per_use + extra)

    def has(self, d):
        return self.loop or 0 <= self.b + d < TILES


def need(eng, sem, value):
    if isinstance(value, int) and value <= 0:
        return
    eng.wait_ge(sem, value)


def build(nc, x, keys, vals, g_attn, g_ffn, rwt, wexp, out):
    with ExitStack() as ctx:
        def sb(name, shape, dt=F32):
            return ctx.enter_context(nc.sbuf_tensor(name, shape, dt))

        def sem(name):
            return ctx.enter_context(nc.semaphore(name))

        q_scr = nc.dram_tensor("q_scr", [PW, PARTS, HR, HPT * D], F32, kind="Internal").ap()
        k_scr = nc.dram_tensor("k_scr", [PW, PARTS, HR, HPT * D], F32, kind="Internal").ap()
        r_scr = nc.dram_tensor("r_scr", [PW, HPT, D], F32, kind="Internal").ap()
        o_scr = nc.dram_tensor("o_scr", [PW, J * P, D], F32, kind="Internal").ap()
        x_rows = nc.dram_tensor("x_rows", [DUMMY + P, ROW], F32, kind="Internal").ap()
        sums_dram = [nc.dram_tensor(f"sums{q}", [ZR * (TILES - TURNS_FIRST), D], F32, kind="Internal").ap()
                     for q in range(NS)]

        X = sb("X", [P, TILES + 2, D])
        XN = sb("XN", [P, PW, D])
        QS = sb("QS", [P, PW, PARTS, D], F32R)
        KR = sb("KR", [P, PW, D])
        KS = sb("KS", [P, PW, PARTS, D], F32R)
        V = sb("V", [P, PW, MT, VW])
        PE_T = sb("PE_T", [P, EXP_RING, MT * D])
        MX = sb("MX", [P, 2, HPT // 2 * MT])
        MXT = sb("MXT", [HPT // 2 * MT, 2, PARTS, P], F32R)
        O4 = sb("O4", [P, PW, J, D])
        OC = sb("OC", [P, PW, D])
        SM = sb("SM", [P, PW, HPT * D // P])
        DN = sb("DN", [P, PW, D])
        OM = sb("OM", [P, PW, D])
        ST1 = sb("ST1", [P, PW, 6])
        MV1 = sb("MV1", [P, PW, 2])
        RS1 = sb("RS1", [P, PW, 2])
        ST2 = sb("ST2", [P, PW, 6])
        MV2 = sb("MV2", [P, PW, 2])
        RS2 = sb("RS2", [P, PW, 2])
        XN2 = sb("XN2", [P, PW, ROW])
        XT2 = sb("XT2", [P, PW, D])
        RW = sb("RW", [P, MT, E])
        NM = sb("NM", [P, PW, 1])
        EX = sb("EX", [P, PW, E])
        SE = sb("SE", [P, PW, 1])
        RSE = sb("RSE", [P, PW, 1])
        PR = sb("PR", [P, PW, E])
        TOP = sb("TOP", [P, PW, K8])
        REST = sb("REST", [P, PW, E])
        MASK = sb("MASK", [P, PW, E], BF16)
        SEEN = sb("SEEN", [P, PW, E], BF16)
        SL = sb("SL", [P, PW, E])
        SLM = sb("SLM", [P, PW, E])
        S8 = sb("S8", [P, PW, K8])
        IDX = sb("IDX", [P, PW, K8], I32)
        TG = sb("TG", [P, 2])
        GIN = sb("GIN", [P, 2])
        IDENT = sb("IDENT", [P, P])
        UPPER = sb("UPPER", [P, P], BF16)
        ONES = sb("ONES", [P, P], BF16)
        ONESF = sb("ONESF", [E, P])
        NHALF = sb("NHALF", [P, 1])
        IOTI = sb("IOTI", [P, E], I32)
        BASE1 = sb("BASE1", [P, E])
        ZERO = sb("ZERO", [P, D])
        FILL = sb("FILL", [P, 2, ROW])
        TOKEN = sb("TOKEN", [P, TILES], I32)
        NI_I = sb("NI_I", [E, NO], I32)
        NI = sb("NI", [E, NO])
        EI_I = sb("EI_I", [E, 2], I32)
        EI = sb("EI", [E, 2])
        CNT = sb("CNT", [E, 8])
        CNI = sb("CNI", [E, 2], I32)
        NTB = sb("NTB", [E, 1], BF16)
        A1 = PE_T[0:E, 8, 0:NO]
        A2 = PE_T[0:E, 8, NO:2 * NO]
        RB = PE_T[0:E, 9, 0:NO]
        TB = PE_T[0:E, 10, 0:TAB_N]
        TABF = PE_T[0:1, 11, 0:TAB_N]
        TAB = PE_T[0:1, 8, 0:TAB_N].bitcast(I32)
        EXPS = PE_T.rearrange("p a b -> p (a b)")

        def exps(at, n, d):
            return EXPS[:, at:at + n * d].rearrange("p (n d) -> p n d", d=d)

        XET = exps(0, 2 * MT, MAIN).rearrange("p (b k) m -> p b k m", k=MT)
        SG = exps(2 * MT * MAIN, 2, MAIN)
        HT = exps(2 * MT * MAIN + 2 * MAIN, 2, MAIN)
        Y = exps(2 * MT * MAIN + 4 * MAIN, 2 * NJ, D).rearrange("p (b j) d -> p b j d", j=NJ)
        with ExitStack() as attention:
            Q = attention.enter_context(nc.sbuf_tensor("Q", [MAXR + PARTS, PW, HPT, D], F32R))
            K = attention.enter_context(nc.sbuf_tensor("K", [MAXR + PARTS, PW, HPT, D], F32R))
        with ExitStack() as experts:
            W = experts.enter_context(nc.sbuf_tensor("W", [P, SLOTS, WCOLS], F32))
            XE = experts.enter_context(nc.sbuf_tensor("XE", [P, SLOTS, NJ, ROW], F32))
            WP = experts.enter_context(nc.sbuf_tensor("WP", [P, WS, PARTS, WCOLS], F32R))
            XTP = experts.enter_context(nc.sbuf_tensor("XTP", [P, 2, PARTS, MT, MAIN], F32R))
            HP = experts.enter_context(nc.sbuf_tensor("HP", [P, 2, PARTS, MAIN], F32R))
        ACC = sb("ACC", [P, FS, NS, D])
        OT = sb("OT", [P, FS, D])

        SC = ctx.enter_context(nc.psum_tensor("SC", [P, 2, 2, 512], F32))
        ST = ctx.enter_context(nc.psum_tensor("ST", [P, 3, 512], F32))
        OX = ctx.enter_context(nc.psum_tensor("OX", [P, 512], F32))

        MISC = ST[:, 2, :]
        MISC_MAX = MISC[0:16, 0:P]
        MISC_E = MISC[:, P:P + E]
        MISC_XT = MISC[:, P + E:P + E + D]

        XP = ST[:, 0:MT, 0:MAIN]
        GU = SC[:, :, :, 0:MAIN]
        YP = [ST[:, 2, 0:D], ST[:, 2, D:2 * D], OX[:, 0:D]]

        x_in = [sem(f"x_in{n}") for n in range(4)]
        gates_in = sem("gates_in")
        router_in = sem("router_in")
        kr_in = [sem(f"kr_in{n}") for n in range(PW)]
        k_out = [sem(f"k_out{n}") for n in range(PW)]
        k_in = [sem(f"k_in{n}") for n in range(PW)]
        v_in = [sem(f"v_in{n}") for n in range(PW)]
        q_out = [sem(f"q_out{n}") for n in range(PW)]
        q_in = [sem(f"q_in{n}") for n in range(PW)]
        max_in = [sem(f"max_in{n}") for n in range(2)]
        o_out = [sem(f"o_out{n}") for n in range(PW)]
        o_in = [sem(f"o_in{n}") for n in range(PW)]
        s_in = [sem(f"s_in{n}") for n in range(PW)]
        r_out = [sem(f"r_out{n}") for n in range(PW)]
        r_in = [sem(f"r_in{n}") for n in range(PW)]
        dispatched = [sem(f"dispatched{n}") for n in range(PW)]
        pool_const = sem("pool_const")
        dve_const = sem("dve_const")
        q_zero = sem("q_zero")
        k_zero = sem("k_zero")
        k_ones = sem("k_ones")
        tanh_done = sem("tanh_done")
        ln1 = sem("ln1")
        rstd1 = sem("rstd1")
        norm1 = sem("norm1")
        k_high = sem("k_high")
        k_low = sem("k_low")
        scored = sem("scored")
        max_done = sem("max_done")
        misc_a = sem("misc_a")
        misc_b = sem("misc_b")
        mxt_high = sem("mxt_high")
        mxt_low = sem("mxt_low")
        st_done = sem("st_done")
        exp_done = sem("exp_done")
        pv_done = sem("pv_done")
        o_copied = sem("o_copied")
        inverted = sem("inverted")
        att = sem("att")
        om_done = sem("om_done")
        rstd2 = sem("rstd2")
        norm2 = sem("norm2")
        xt_copied = sem("xt_copied")
        route = sem("route")
        rexp = sem("rexp")
        place = sem("place")
        held = [sem(f"held_{n}") for n in ("sp", "dve", "pool", "act")]
        tab_pe = sem("tab_pe")
        tab_dve = sem("tab_dve")
        filled = [sem(f"filled{c}") for c in range(3)]
        sums_zero = sem("sums_zero")
        w_in = [sem(f"w_in{n}") for n in range(SLOTS)]
        xe_in = [sem(f"xe_in{n}") for n in range(SLOTS)]
        xt_ps = sem("xt_ps")
        xt_high = sem("xt_high")
        xt_low = sem("xt_low")
        w_high = sem("w_high")
        w_low = sem("w_low")
        gu_ps = sem("gu_ps")
        silu_done = sem("silu_done")
        h_done = sem("h_done")
        h_high = sem("h_high")
        h_low = sem("h_low")
        y_ps = sem("y_ps")
        y_weighted = sem("y_weighted")
        added = [sem(f"added{q}") for q in range(NS)]
        o_free = sem("o_free")
        o_fill = sem("o_fill")
        o_loaded = sem("o_loaded")
        o_xt_ps = sem("o_xt_ps")
        o_xet = sem("o_xet")
        o_gu_ps = sem("o_gu_ps")
        o_silu = sem("o_silu")
        o_h = sem("o_h")
        o_y_ps = sem("o_y_ps")
        o_weighted = sem("o_weighted")
        o_added = sem("o_added")
        acc_in = [sem(f"acc_in{n}") for n in range(FS // 2)]
        summed = sem("summed")
        stored = [sem(f"stored{n}") for n in range(FS // 2)]

        SP_H, DVE_H, POOL_H, ACT_H = held

        def hold(eng, own, s, value):
            if isinstance(value, int):
                need(eng, s, value)
            else:
                eng.wait_ge(s, value)
                eng.sem_inc(own, 1)

        FIRST_FILLS = 4
        FILLS = 2 * E // 4 + E // 8 + 1
        assert SLOTS * NJ % NS == 0

        def added_up_to(i, n, j):
            c = n * NJ + j
            return added[c % NS], (i * (SLOTS * NJ // NS) + (c // NS + 1)) * 16

        def more(i, n):
            return not isinstance(i, int) or i * SLOTS + n < E

        UNITS = HPT // 2
        def ahead(T):
            return T.loop or T.b < TILES

        n_full = (TILES - TURNS_FIRST) // PW
        assert n_full * PW == TILES - TURNS_FIRST

        def turns(eng, body):
            for t in range(TURNS_FIRST):
                body(Turn(0, t))
            with eng.Fori(0, n_full) as i:
                for s in range(PW):
                    body(Turn(i, TURNS_FIRST + s))
            for t in range(TILES, TILES + LAST):
                body(Turn(0, t))

        block = ctx.enter_context(nc.Block())

        @block.sync
        def _(sp):
            xt = x.rearrange("(t p) d -> p t d", p=P)
            sp.dma_start(X[:, 0:2, :], xt[:, 0:2, :]).then_inc(x_in[0], 16)
            sp.dma_start(KR[:, 0], keys[0]).then_inc(kr_in[0], 16)
            sp.dma_start(KR[:, 1], keys[1]).then_inc(kr_in[1], 16)
            sp.dma_start(KR[:, 2], keys[2]).then_inc(kr_in[2], 16)
            sp.dma_start(GIN[:, 0:1], bass.AP(g_attn.tensor, 0, [[0, P], [1, 1]])).then_inc(gates_in, 16)
            sp.dma_start(GIN[:, 1:2], bass.AP(g_ffn.tensor, 0, [[0, P], [1, 1]])).then_inc(gates_in, 16)

            def part_write(T, d, scr, parts, out_sem, ready, per_tile):
                s = T.slot(d)
                hold(sp, SP_H, ready, T.count(d, per_tile, per_tile))
                sp.dma_start(scr[s].rearrange("a c (n d) -> a (c n) d", d=D).rearrange("a p d -> p a d"),
                             parts[:, s].bitcast(F32)).then_inc(out_sem[s], 16)

            def rows_zeroed(T, d, zeroed):
                if not T.loop and T.b + d < PW:
                    sp.wait_ge(zeroed, T.b + d + 1)

            def q_read(T, d):
                s = T.slot(d)
                rows_zeroed(T, d, q_zero)
                hold(sp, SP_H, st_done, T.count(d - 2, HPT, 0))
                hold(sp, SP_H, q_out[s], T.slot_count(d, 16))
                for n in range(2):
                    sp.dma_start(Q[16 * n:16 * n + 16, s].bitcast(F32).rearrange("p n d -> p (n d)"),
                                 q_scr[s].rearrange("a c m -> (a c) m")).then_inc(q_in[s], 16)

            def k_read(T, d):
                s = T.slot(d)
                rows_zeroed(T, d, k_zero)
                hold(sp, SP_H, st_done, T.count(d - 2, HPT, 0))
                hold(sp, SP_H, k_out[s], T.slot_count(d, 16))
                rows = k_scr[s].rearrange("a c m -> (a c) m")
                for to, of, n in ((0, 0, 16), (16, 8, 8), (24, 0, 8)):
                    sp.dma_start(K[to:to + n, s].bitcast(F32).rearrange("p n d -> p (n d)"), rows[of:of + n, :]
                                 ).then_inc(k_in[s], 16)

            def max_load(T, d, h):
                hold(sp, SP_H, mxt_low, T.count(d, 2, h + 1))
                for a in range(PARTS):
                    sp.dma_start(Q[MAXR + a:MAXR + a + 1, T.slot(d), HPT // 2 * h:HPT // 2 * (h + 1), :].bitcast(F32),
                                 MXT[:, h, a, :].bitcast(F32)).then_inc(max_in[h], 16)

            sp.wait_ge(dve_const, 4)
            sp.dma_start(K[MAXR:].bitcast(F32).rearrange("p s n d -> p (s n d)"),
                         bass.AP(ONESF[:, :].tensor, 0, [[P, PARTS], [0, PW * HPT * D // P], [1, P]])).then_inc(k_ones, 16)
            T0 = Turn(0, 0)
            part_write(T0, 0, k_scr, KS, k_out, k_low, 1)
            part_write(T0, 0, q_scr, QS, q_out, ln1, 4)
            k_read(T0, 0)
            q_read(T0, 0)
            part_write(T0, 1, k_scr, KS, k_out, k_low, 1)
            part_write(T0, 1, q_scr, QS, q_out, ln1, 4)
            sp.dma_start(V[:, 0], vals[0]).then_inc(v_in[0], 16)
            sp.dma_start(RW[:, :, :], rwt.rearrange("(k p) e -> p k e", p=P)).then_inc(router_in, 16)
            sp.dma_start(X[:, 2:4, :], xt[:, 2:4, :]).then_inc(x_in[1], 16)

            def turn(T):
                if ahead(T):
                    k_read(T, 1)
                    q_read(T, 1)
                    s3 = T.slot(3)
                    hold(sp, SP_H, k_low, T.count(1, 1, 0))
                    sp.dma_start(KR[:, s3], keys[bass.ds(T.tile(3), 1)] if T.loop else keys[T.b + 3]
                                 ).then_inc(kr_in[s3], 16)
                if not T.loop and T.b in (1, 3):
                    a, b = (4, 8) if T.b == 1 else (8, TILES)
                    sp.dma_start(X[:, a:b, :], xt[:, a:b, :]).then_inc(x_in[2 + T.b // 2], 16)
                if T.has(-1):
                    max_load(T, -1, 1)
                if T.has(-2):
                    s = T.slot(-2)
                    hold(sp, SP_H, o_copied, T.count(-2, J, J))
                    sp.dma_start(o_scr[s].rearrange("(j p) d -> p j d", p=P), O4[:, s]).then_inc(o_out[s], 16)
                if ahead(T):
                    s1 = T.slot(1)
                    hold(sp, SP_H, pv_done, T.count(-1, J, 0))
                    sp.dma_start(V[:, s1], vals[bass.ds(T.tile(1), 1)] if T.loop else vals[T.b + 1]
                                 ).then_inc(v_in[s1], 16)
                    part_write(T, 2, k_scr, KS, k_out, k_low, 1)
                if T.has(-2):
                    hold(sp, SP_H, o_out[s], T.slot_count(-2, 16))
                    sp.dma_start(SM[:, s, :], bass.AP(o_scr.tensor, (s * J * P + HR) * D,
                                                      [[32 * D, HPT], [1, D]])).then_inc(s_in[s], 16)
                    rows = o_scr[s].rearrange("(n r) d -> r n d", r=32)
                    hold(sp, SP_H, om_done, T.count(-4, 1, 0))
                    sp.dma_start(OC[:, s, :], rows[0:HR]).then_inc(o_in[s], 16)
                if T.has(0):
                    max_load(T, 0, 0)
                if ahead(T):
                    part_write(T, 2, q_scr, QS, q_out, ln1, 4)
                if T.has(-2):
                    hold(sp, SP_H, inverted, T.count(-2, 1, 1))
                    sp.dma_start(r_scr[s].rearrange("n d -> (n d)").rearrange("(p f) -> p f", p=P), SM[:, s, :]
                                 ).then_inc(r_out[s], 16)
                    hold(sp, SP_H, r_out[s], T.slot_count(-2, 16))
                    sp.dma_start(DN[:, s, :], bass.AP(r_scr.tensor, s * HPT * D, [[0, HR], [D, HPT], [1, D]])
                                 ).then_inc(r_in[s], 16)
                if T.loop:
                    for q in range(NS):
                        sp.dma_start(sums_dram[q][bass.ds((T.tile(0) - TURNS_FIRST) * ZR, ZR), :].rearrange(
                                         "(p a) d -> p a d", p=P),
                                     bass.AP(ZERO[:, :].tensor, 0, [[D, P], [0, ZR // P], [1, D]])
                                     ).then_inc(sums_zero, 16)

            turns(sp, turn)
            for n in range(PW):
                sp.wait_ge(kr_in[n], 16 * len(range(n, TILES + 3, PW)))
                sp.wait_ge(k_in[n], 48 * len(range(n, TILES + 1, PW)))
                sp.wait_ge(q_in[n], 32 * len(range(n, TILES + 1, PW)))
                sp.wait_ge(v_in[n], 16 * len(range(n, TILES + 1, PW)))
                sp.wait_ge(k_out[n], 16 * len(range(n, TILES + 2, PW)))
                sp.wait_ge(q_out[n], 16 * len(range(n, TILES + 2, PW)))

            def load_weights(i, n):
                e = i * SLOTS + n
                sp.dma_start(W[:, n, :], wexp[bass.ds(e, 1)].rearrange("a p c -> (a p) c")).then_inc(w_in[n], 16)

            def load_rows(i, n):
                e = i * SLOTS + n
                sp.dma_start(XE[:, n, 0:2, :].rearrange("p j c -> p (j c)"),
                             x_rows[bass.ds(e * CAP, 2 * P), :].rearrange("(p j) c -> p (j c)", j=2)
                             ).then_inc(xe_in[n], 16)
                sp.dma_start(XE[0:ROWS_J[2], n, 2, :], x_rows[bass.ds(e * CAP + 2 * P, ROWS_J[2]), :]
                             ).then_inc(xe_in[n], 16)

            for n in range(SLOTS):
                load_weights(0, n)
            for n in range(PW):
                sp.wait_ge(dispatched[n], 16 * K8 * len(range(n, TILES, PW)))
            for n in range(SLOTS):
                load_rows(0, n)
            sp.wait_ge(tab_dve, TAB_OPS)
            over = sp.value_load(TAB[0:1, TAB_N - 1:TAB_N], min_val=0, max_val=NO)
            with sp.Fori(1, E // SLOTS) as i:
                for n in range(SLOTS):
                    for j in range(NJ):
                        hold(sp, SP_H, *added_up_to(i, n - SLOTS, j))
                    load_weights(i, n)
                    load_rows(i, n)

            for q in range(NS):
                sp.wait_ge(added[q], 16 * E * NJ // NS)
            with sp.If(over > 0):
                with sp.Fori(0, E) as e:
                    r = sp.value_load(TAB[0:1, bass.ds(e + 2 * NO, 1)], min_val=0, max_val=DUMMY - P)
                    sp.dma_start(x_rows[bass.ds(r, P), :], FILL[:, 0, :]).then_inc(o_fill, 16)
                sp.wait_ge(o_fill, 16 * E)
                with sp.Fori(0, NO) as i:
                    r = sp.value_load(TAB[0:1, bass.ds(i, 1)], min_val=0, max_val=DUMMY)
                    e = sp.value_load(TAB[0:1, bass.ds(i + NO, 1)], min_val=0, max_val=E - 1)
                    hold(sp, SP_H, o_free, i + 1)
                    sp.dma_start(XE[:, 0, 0, :], x_rows[bass.ds(r, P), :]).then_inc(o_loaded, 16)
                    sp.dma_start(W[:, 0, :], wexp[bass.ds(e, 1)].rearrange("a p c -> (a p) c")
                                 ).then_inc(o_loaded, 16)
                sp.wait_ge(o_added, 16 * NO)

            def load_sums(i, h):
                if not (isinstance(i, int) and i == 0):
                    hold(sp, SP_H, summed, (i * FS + (2 * h + 2 - FS)) * NS)
                for q in range(NS):
                    rows = sums_dram[q][bass.ds((i * FS + 2 * h) * P, 2 * P), :]
                    sp.dma_start(ACC[:, 2 * h:2 * h + 2, q, :], rows.rearrange("(a p) d -> p a d", p=P)
                                 ).then_inc(acc_in[h], 16)

            for h in range(FS // 2):
                load_sums(0, h)
            with sp.Fori(1, TILES // FS) as i:
                for h in range(FS // 2):
                    load_sums(i, h)
            for h in range(FS // 2):
                sp.wait_ge(stored[h], 16 * TILES // FS)

        @block.gpsimd
        def _(pool):
            nc.gpsimd.memset(IDENT[:, :], 0.0).then_inc(pool_const, 1)
            nc.gpsimd.memset(UPPER[:, :], 1.0).then_inc(pool_const, 1)
            nc.gpsimd.memset(ONES[:, :], 1.0).then_inc(pool_const, 1)
            nc.gpsimd.memset(NHALF[:, :], -0.5).then_inc(pool_const, 1)
            nc.gpsimd.iota(IOTI[:, :], pattern=[[CAP, E]], base=1, channel_multiplier=0).then_inc(pool_const, 1)
            nc.gpsimd.memset(FILL[:, :, :], 0.0).then_inc(pool_const, 1)
            nc.gpsimd.iota(TOKEN[:, :], pattern=[[P, TILES]], base=0, channel_multiplier=1).then_inc(pool_const, 1)
            nc.gpsimd.iota(NI_I[:, :], pattern=[[1, NO]], base=0, channel_multiplier=0).then_inc(pool_const, 1)
            nc.gpsimd.iota(EI_I[:, 0:1], pattern=[[1, 1]], base=0, channel_multiplier=1).then_inc(pool_const, 1)
            nc.gpsimd.iota(EI_I[:, 1:2], pattern=[[1, 1]], base=0, channel_multiplier=CAP).then_inc(pool_const, 1)
            pool.wait_ge(pool_const, 10)
            for n in range(2):
                nc.gpsimd.iota(FILL[:, n, ROW - 1:ROW].bitcast(I32), pattern=[[1, 1]], base=TOK,
                               channel_multiplier=1).then_inc(pool_const, 1)
            nc.gpsimd.affine_select(out=IDENT[:, :], in_=IDENT[:, :], compare_op=ALU.not_equal, fill=1.0, base=0,
                                    pattern=[[-1, P]], channel_multiplier=1).then_inc(pool_const, 1)
            nc.gpsimd.affine_select(out=UPPER[:, :], in_=UPPER[:, :], compare_op=ALU.is_gt, fill=0.0, base=0,
                                    pattern=[[1, P]], channel_multiplier=-1).then_inc(pool_const, 1)
            pool.wait_ge(pool_const, 14)

            def fill(n):
                if n < 2 * E // 4:
                    c, n = divmod(n, E // 4)
                    return pool.dma_start(
                        bass.AP(x_rows.tensor, (4 * n * CAP + c * P) * ROW, [[2 * ROW, P // 2], [CAP * ROW, 4], [1, 2 * ROW]]),
                        bass.AP(FILL[:, :, :].tensor, c * (P // 2) * 2 * ROW, [[2 * ROW, P // 2], [0, 4], [1, 2 * ROW]])
                        ).then_inc(filled[c], 16)
                n -= 2 * E // 4
                if n < E // 8:
                    return pool.dma_start(
                        bass.AP(x_rows.tensor, (8 * n * CAP + 2 * P) * ROW,
                                [[ROW, ROWS_J[2]], [CAP * ROW, 8], [1, ROW]]),
                        bass.AP(FILL[:, :, :].tensor, 0, [[2 * ROW, ROWS_J[2]], [0, 8], [1, ROW]])).then_inc(filled[2], 16)
                return pool.dma_start(x_rows[DUMMY:DUMMY + P, :], FILL[:, 0, :]).then_inc(filled[2], 16)

            def deviation(T, d, mv, rs, ready, at, per_tile, done):
                s = T.slot(d)
                need(pool, ready, T.count(d, per_tile, at))
                nc.gpsimd.tensor_tensor(rs[:, s, 0:1], mv[:, s, 1:2], NHALF[:, :], ALU.pow).then_inc(done, 1)
                hold(pool, POOL_H, done, T.count(d, 2, 1))
                nc.gpsimd.tensor_scalar(rs[:, s, 1:2], mv[:, s, 0:1], rs[:, s, 0:1], -1.0, ALU.mult, ALU.mult
                                        ).then_inc(done, 1)

            def key_low(T, d):
                s = T.slot(d)
                if T.has(d - PW):
                    need(pool, k_out[s], T.slot_count(d - PW, 16))
                need(pool, k_high, T.count(d, 1, 1))
                nc.gpsimd.tensor_tensor(KS[:, s, 1], KR[:, s], KS[:, s, 0].bitcast(F32), ALU.subtract
                                        ).then_inc(k_low, 1)

            def fills(T, k):
                if not T.loop and T.b < TURNS_FIRST:
                    first, end = (FIRST_FILLS + (FILLS - FIRST_FILLS) * t // TURNS_FIRST for t in (T.b, T.b + 1))
                    for n in range(first + k, min(first + k + 2, end)):
                        pool.wait_ge(scored, UNITS * T.b + (n - first) + 1)
                        fill(n)

            def dispatch(T, a, b):
                if T.has(-5):
                    s = T.slot(-5)
                    if a == 0:
                        if T.b in (5, 6) and not T.loop:
                            pool.wait_ge(filled[T.b - 5], 16 * E // 4)
                        hold(pool, POOL_H, place, T.count(-5, 5, 5))
                    for k in range(a, b):
                        pool.indirect_dma_start(x_rows, bass.IndirectOffsetOnAxis(ap=IDX[:, s, k:k + 1], axis=0),
                                                XN2[:, s, :], None).then_inc(dispatched[s], 16)

            for n in range(FIRST_FILLS):
                fill(n)
            key_low(Turn(0, 0), 0)
            deviation(Turn(0, 0), 0, MV1, RS1, ln1, 3, 4, rstd1)
            key_low(Turn(0, 0), 1)
            deviation(Turn(0, 0), 1, MV1, RS1, ln1, 3, 4, rstd1)
            for n in range(1, PW):
                pool.wait_ge(k_zero, n)
                nc.gpsimd.memset(K[0:MAXR, n].bitcast(F32), 0.0).then_inc(k_zero, 1)

            def turn(T):
                if T.has(-3):
                    s = T.slot(-3)
                    need(pool, o_in[s], T.slot_count(-3, 16))
                    need(pool, r_in[s], T.slot_count(-3, 16))
                    nc.gpsimd.tensor_tensor(OM[:, s], OC[:, s], DN[:, s], ALU.mult).then_inc(om_done, 1)
                if ahead(T):
                    deviation(T, 2, MV1, RS1, ln1, 3, 4, rstd1)
                    key_low(T, 2)
                fills(T, 0)
                dispatch(T, 0, 3)
                fills(T, 2)
                if T.has(-3):
                    deviation(T, -3, MV2, RS2, att, 4, 4, rstd2)
                dispatch(T, 3, 8)
                fills(T, 4)
                if not T.loop and T.b == 6:
                    pool.wait_ge(filled[2], 16 * (E // 8 + 1))

            turns(pool, turn)

            pool.wait_ge(tab_dve, TAB_OPS)
            pool.wait_ge(sums_zero, 16 * NS * (TILES - TURNS_FIRST))
            over = pool.value_load(TAB[0:1, TAB_N - 1:TAB_N], min_val=0, max_val=NO)

            def add_expert(i, n):
                e = i * SLOTS + n
                for j in range(NJ):
                    sum_added, count = added_up_to(i, n, j)
                    if not isinstance(count, int) or count > 16:
                        hold(pool, POOL_H, sum_added, count - 16)
                    hold(pool, POOL_H, y_weighted, e * NJ + (j + 1))
                    m = ROWS_J[j]
                    pool.indirect_dma_start(
                        sums_dram[(n * NJ + j) % NS],
                        bass.IndirectOffsetOnAxis(ap=XE[0:m, n, j, ROW - 1:ROW].bitcast(I32), axis=0),
                        Y[0:m, n % 2, j, :], None, compute_op=ALU.add).then_inc(sum_added, 16)

            for n in range(SLOTS):
                add_expert(0, n)
            with pool.Fori(1, E // SLOTS) as i:
                for n in range(SLOTS):
                    add_expert(i, n)
            with pool.If(over > 0):
                pool.sem_inc(o_free, 1)
                with pool.Fori(0, NO) as i:
                    hold(pool, POOL_H, o_weighted, i + 1)
                    pool.indirect_dma_start(
                        sums_dram[0], bass.IndirectOffsetOnAxis(ap=XE[:, 0, 0, ROW - 1:ROW].bitcast(I32), axis=0),
                        Y[:, 0, 0, :], None, compute_op=ALU.add).then_inc(o_added, 16)
                    hold(pool, POOL_H, o_added, i * 16 + 16)
                    pool.sem_inc(o_free, 1)

        @block.vector
        def _(dve):
            nc.vector.memset(ZERO[:, :], 0.0).then_inc(dve_const, 1)
            nc.vector.memset(Q[0:MAXR, 0].bitcast(F32), 0.0).then_inc(q_zero, 1)
            nc.vector.memset(X[:, TILES:TILES + 2, :], 0.0).then_inc(dve_const, 1)
            nc.vector.memset(SEEN[:, 0, :], 0.0).then_inc(dve_const, 1)
            nc.vector.memset(ONESF[:, :], 1.0).then_inc(dve_const, 1)
            dve.wait_ge(pool_const, 10)
            nc.vector.tensor_copy(BASE1[:, :], IOTI[:, :]).then_inc(dve_const, 1)
            nc.vector.tensor_copy(NI[:, :], NI_I[:, :]).then_inc(dve_const, 1)
            nc.vector.tensor_copy(EI[:, :], EI_I[:, :]).then_inc(dve_const, 1)
            dve.wait_ge(dve_const, 7)

            def ln1_stats(t):
                nc.vector.bn_stats(ST1[:, t], X[:, t, :]).then_inc(ln1, 1)
                dve.wait_ge(ln1, 4 * t + 1)
                nc.vector.bn_aggr(MV1[:, t], ST1[:, t]).then_inc(ln1, 1)
                dve.wait_ge(ln1, 4 * t + 2)
                nc.vector.tensor_scalar(MV1[:, t, 1:2], MV1[:, t, 1:2], EPS, None, ALU.add).then_inc(ln1, 1)

            def q_low(T, d):
                s = T.slot(d)
                if T.has(d - PW):
                    need(dve, q_out[s], T.slot_count(d - PW, 16))
                need(dve, norm1, T.count(d, 2, 2))
                nc.vector.tensor_tensor(QS[:, s, 1], XN[:, s], QS[:, s, 0].bitcast(F32), ALU.subtract
                                        ).then_inc(ln1, 1)

            def take_max(T, u):
                h = u // 4
                pair = u % 2
                if u % 4 == 0:
                    need(dve, misc_b if h == 0 else misc_a, T.count(0, 1, 0))
                need(dve, scored, T.count(0, UNITS, u + 1))
                nc.vector.tensor_reduce(MX[:, h, 4 * (u % 4):4 * (u % 4) + 4],
                                        SC[:, pair, :, :].rearrange("p a (m n) -> p (a m) n", m=MT),
                                        axis=AX_X, op=ALU.max, negate=True).then_inc(max_done, 1)

            def max_low(T, d, h):
                need(dve, mxt_high, T.count(d, 2, h + 1))
                nc.vector.tensor_tensor(MXT[:, h, 1, :], MISC_MAX, MXT[:, h, 0, :].bitcast(F32),
                                        ALU.subtract).then_inc(mxt_low, 1)

            def ma(T):
                if T.has(-4):
                    need(dve, xt_copied, T.count(-4, 1, 1))
                if T.has(-1):
                    max_low(T, -1, 1)
                if T.has(-5):
                    need(dve, misc_a, T.count(0, 1, 0))
                    s = T.slot(-5)
                    nc.vector.tensor_tensor(SL[:, s], MISC_E, BASE1[:, :], ALU.add).then_inc(place, 1)

            def mb(T):
                if T.has(0):
                    max_low(T, 0, 0)
                if T.has(-4):
                    need(dve, misc_b, T.count(0, 1, 1))
                    s = T.slot(-4)
                    nc.vector.tensor_reduce(NM[:, s], MISC_E, axis=AX_X, op=ALU.max,
                                            negate=True).then_inc(route, 1)

            def route_rest(T):
                s = T.slot(-4)
                need(dve, rexp, T.count(-4, 1, 1))
                nc.vector.reciprocal(RSE[:, s], SE[:, s]).then_inc(route, 1)
                need(dve, route, T.count(-4, 8, 2))
                nc.vector.tensor_scalar(PR[:, s], EX[:, s], RSE[:, s], None, ALU.mult).then_inc(route, 1)
                hold(dve, DVE_H, route, T.count(-4, 8, 3))
                nc.vector.max(TOP[:, s], PR[:, s]).then_inc(route, 1)
                hold(dve, DVE_H, route, T.count(-4, 8, 4))
                nc.vector.match_replace(REST[:, s], TOP[:, s], PR[:, s], -1.0).then_inc(route, 1)
                need(dve, route, T.count(-4, 8, 5))
                nc.vector.tensor_scalar(MASK[:, s], REST[:, s], 0.0, None, ALU.is_lt).then_inc(route, 1)
                need(dve, route, T.count(-4, 8, 6))
                nc.vector.tensor_tensor(XN2[:, s, D:D + E], PR[:, s], MASK[:, s], ALU.mult).then_inc(route, 1)
                nc.vector.tensor_tensor(SEEN[:, T.slot(-3)], SEEN[:, s], MASK[:, s], ALU.add).then_inc(route, 1)

            def x_at(T, d):
                at = T.tile(d)
                return X[:, bass.ds(at, 1), :].rearrange("p a d -> p (a d)") if T.loop else X[:, at, :]

            def invert(T):
                s = T.slot(-2)
                need(dve, s_in[s], T.slot_count(-2, 16))
                nc.vector.reciprocal(SM[:, s], SM[:, s]).then_inc(inverted, 1)

            dve.wait_ge(x_in[0], 16)
            for n in range(2):
                ln1_stats(n)
                q_low(Turn(0, 0), n)
            nc.vector.memset(Q[0:MAXR, 1].bitcast(F32), 0.0).then_inc(q_zero, 1)
            dve.wait_ge(tanh_done, 1)

            def middle(T):
                s1, s2, s3 = T.slot(2), T.slot(-3), T.slot(-5)
                if ahead(T):
                    if not T.loop and T.b in (0, 2, 6):
                        dve.wait_ge(x_in[1 + (T.b + 1) // 3], 16)
                    nc.vector.bn_stats(ST1[:, s1], x_at(T, 2)).then_inc(ln1, 1)
                if T.has(-3):
                    need(dve, om_done, T.count(-3, 1, 1))
                    nc.vector.scalar_tensor_tensor(out=x_at(T, -3), in0=OM[:, s2], scalar=TG[:, 0:1], in1=x_at(T, -3),
                                                   op0=ALU.mult, op1=ALU.add).then_inc(att, 1)
                if T.has(-5):
                    need(dve, place, T.count(-5, 5, 1))
                    nc.vector.tensor_tensor(SLM[:, s3], SL[:, s3], MASK[:, s3], ALU.mult).then_inc(place, 1)
                if ahead(T):
                    hold(dve, DVE_H, ln1, T.count(2, 4, 1))
                    nc.vector.bn_aggr(MV1[:, s1], ST1[:, s1]).then_inc(ln1, 1)
                if T.has(-3):
                    hold(dve, DVE_H, att, T.count(-3, 4, 1))
                    nc.vector.bn_stats(ST2[:, s2], x_at(T, -3)).then_inc(att, 1)
                if T.has(-5):
                    hold(dve, DVE_H, place, T.count(-5, 5, 2))
                    nc.vector.max(S8[:, s3], SLM[:, s3]).then_inc(place, 1)
                if ahead(T):
                    need(dve, ln1, T.count(2, 4, 2))
                    nc.vector.tensor_scalar(MV1[:, s1, 1:2], MV1[:, s1, 1:2], EPS, None, ALU.add).then_inc(ln1, 1)
                if T.has(-3):
                    hold(dve, DVE_H, att, T.count(-3, 4, 2))
                    nc.vector.bn_aggr(MV2[:, s2], ST2[:, s2]).then_inc(att, 1)
                if T.has(-5):
                    need(dve, place, T.count(-5, 5, 3))
                    nc.vector.tensor_scalar(IDX[:, s3], S8[:, s3], -1.0, None, ALU.add).then_inc(place, 1)
                    at = T.tile(-5)
                    nc.vector.tensor_copy(XN2[:, s3, ROW - 1:ROW].bitcast(I32), TOKEN[:, bass.ds(at, 1)]
                                          ).then_inc(place, 1)
                if T.has(-3):
                    need(dve, att, T.count(-3, 4, 3))
                    nc.vector.tensor_scalar(MV2[:, s2, 1:2], MV2[:, s2, 1:2], EPS, None, ALU.add).then_inc(att, 1)

            def turn(T):
                if T.has(0):
                    take_max(T, 0)
                if T.has(0):
                    take_max(T, 1)
                ma(T)
                if T.has(0):
                    take_max(T, 2)
                middle(T)
                if T.has(0):
                    take_max(T, 3)
                    take_max(T, 4)
                mb(T)
                if T.has(0):
                    take_max(T, 5)
                if ahead(T):
                    q_low(T, 2)
                if T.has(-2):
                    invert(T)
                if T.has(0):
                    take_max(T, 6)
                if T.has(-4):
                    route_rest(T)
                if T.has(0):
                    take_max(T, 7)
                if not T.loop and T.b == 0:
                    nc.vector.memset(Q[0:MAXR, 2].bitcast(F32), 0.0).then_inc(q_zero, 1)

            turns(dve, turn)

            n_tab = [0]

            def tab(ins, last=False):
                n_tab[0] += 1
                ins.then_inc(tab_dve, 1)
                if not last:
                    dve.wait_ge(tab_dve, n_tab[0])

            dve.wait_ge(tab_pe, 1)
            tab(nc.vector.tensor_copy(CNT[:, 0:1], SC[0:E, 0, 0, 0:1]))
            tab(nc.vector.tensor_scalar(CNT[:, 7:8], CNT[:, 0:1], float(MAIN), None, ALU.max))
            tab(nc.vector.tensor_scalar(CNI[:, 0:1], CNT[:, 7:8], float(P - 1 - MAIN), None, ALU.add))
            tab(nc.vector.tensor_scalar(CNI[:, 1:2], CNI[:, 0:1], 7, None, ALU.arith_shift_right))
            tab(nc.vector.tensor_copy(CNT[:, 1:2], CNI[:, 1:2]))
            tab(nc.vector.tensor_copy(NTB[:, :], CNI[:, 1:2]))
            dve.wait_ge(tab_pe, 2)
            tab(nc.vector.tensor_copy(CNT[:, 2:3], SC[0:E, 0, 1, 0:1]))
            tab(nc.vector.tensor_tensor(CNT[:, 3:4], CNT[:, 2:3], CNT[:, 1:2], ALU.add))
            tab(nc.vector.tensor_scalar(A1[:, :], NI[:, :], CNT[:, 2:3], None, ALU.is_ge))
            tab(nc.vector.tensor_scalar(A2[:, :], NI[:, :], CNT[:, 3:4], None, ALU.is_lt))
            tab(nc.vector.tensor_tensor(A1[:, :], A1[:, :], A2[:, :], ALU.mult))
            tab(nc.vector.tensor_scalar(RB[:, :], NI[:, :], CNT[:, 2:3], float(P), ALU.subtract, ALU.mult))
            tab(nc.vector.tensor_scalar(RB[:, :], RB[:, :], EI[:, 1:2], float(MAIN - DUMMY), ALU.add, ALU.add))
            tab(nc.vector.tensor_tensor(TB[:, 0:NO], RB[:, :], A1[:, :], ALU.mult))
            tab(nc.vector.tensor_scalar(TB[:, NO:2 * NO], A1[:, :], EI[:, 0:1], None, ALU.mult))
            tab(nc.vector.tensor_tensor(CNT[:, 4:5], CNT[:, 7:8], EI[:, 1:2], ALU.add))
            tab(nc.vector.tensor_scalar(TB[:, 2 * NO:2 * NO + E], IDENT[0:E, 0:E], CNT[:, 4:5], None, ALU.mult))
            tab(nc.vector.tensor_copy(TB[:, 2 * NO + E:TAB_N], CNT[:, 1:2]))
            dve.wait_ge(tab_pe, 3)
            tab(nc.vector.tensor_copy(TABF[:, :], SC[0:1, 1, 0, 0:TAB_N]))
            tab(nc.vector.tensor_scalar(TABF[:, 0:NO], TABF[:, 0:NO], float(DUMMY), None, ALU.add))
            tab(nc.vector.tensor_copy(TAB[:, :], TABF[:, :]))
            assert n_tab[0] == TAB_OPS
            over = dve.value_load(TAB[0:1, TAB_N - 1:TAB_N], min_val=0, max_val=NO)

            def low_rows(i, n):
                e, b = i * SLOTS + n, n % 2
                need(dve, xt_high, e + 1)
                nc.vector.tensor_tensor(XTP[:, b, 1], XP, XTP[:, b, 0].bitcast(F32), ALU.subtract).then_inc(xt_low, 1)

            def low_weights(i, n):
                e, w = i * SLOTS + n, n % WS
                need(dve, w_high, e + 1)
                nc.vector.tensor_tensor(WP[:, w, 1], W[:, n % SLOTS, :], WP[:, w, 0].bitcast(F32), ALU.subtract
                                        ).then_inc(w_low, 1)

            def hidden(i, n):
                e, b = i * SLOTS + n, n % 2
                need(dve, silu_done, e + 1)
                if not (isinstance(i, int) and e < 2):
                    need(dve, h_high, e - 1)
                nc.vector.tensor_tensor(HT[:, b, :], GU[:, b, 1, :], SG[:, b, :], ALU.mult).then_inc(h_done, 1)

            def low_hidden(i, n):
                e, b = i * SLOTS + n, n % 2
                need(dve, h_high, e + 1)
                nc.vector.tensor_tensor(HP[:, b, 1], HT[:, b, :], HP[:, b, 0].bitcast(F32), ALU.subtract
                                        ).then_inc(h_low, 1)

            def expert_step(i, n):
                hidden(i, n)
                if more(i, n + 2):
                    low_rows(i, n + 2)
                low_hidden(i, n)
                if more(i, n + 2):
                    low_weights(i, n + 2)

            for n in range(2):
                low_rows(0, n)
                low_weights(0, n)
            for n in range(SLOTS):
                expert_step(0, n)
            with dve.Fori(1, E // SLOTS - 1) as i:
                for n in range(SLOTS):
                    expert_step(i, n)
            for n in range(SLOTS):
                expert_step(E // SLOTS - 1, n)

            with dve.If(over > 0):
                with dve.Fori(0, NO) as i:
                    need(dve, o_silu, i + 1)
                    nc.vector.tensor_tensor(HT[:, 0, 0:P], GU[:, 0, 1, 0:P], SG[:, 0, 0:P], ALU.mult).then_inc(o_h, 1)
                    need(dve, o_y_ps, i + 1)
                    e = dve.value_load(TAB[0:1, bass.ds(i + NO, 1)], min_val=0, max_val=E - 1)
                    nc.vector.tensor_scalar(Y[:, 0, 0, :], YP[0], XE[:, 0, 0, bass.ds(e + D, 1)], None, ALU.mult
                                            ).then_inc(o_weighted, 1)

            def final(i, n):
                t = i * FS + n
                a = bass.ds(t, 1)
                need(dve, acc_in[n // 2], i * (16 * NS) + 16 * NS)
                for q in range(1, NS):
                    nc.vector.tensor_tensor(ACC[:, n, 0, :], ACC[:, n, 0, :], ACC[:, n, q, :], ALU.add).then_inc(summed, 1)
                    if q < NS - 1:
                        need(dve, summed, t * NS + q)
                if not (isinstance(i, int) and i == 0):
                    need(dve, stored[n // 2], i * 16)
                hold(dve, DVE_H, summed, t * NS + (NS - 1))
                nc.vector.scalar_tensor_tensor(out=OT[:, n:n + 1, :], in0=ACC[:, n, 0:1, :], scalar=TG[:, 1:2],
                                               in1=X[:, a, :], op0=ALU.mult, op1=ALU.add).then_inc(summed, 1)

            for n in range(FS):
                final(0, n)
            with dve.Fori(1, TILES // FS) as i:
                for n in range(FS):
                    final(i, n)

        @block.scalar
        def _(act):
            act.wait_ge(gates_in, 32)
            nc.scalar.activation(TG[:, :], GIN[:, :], ACT.Tanh).then_inc(tanh_done, 1)

            def x_at(T, d):
                at = T.tile(d)
                return X[:, bass.ds(at, 1), :].rearrange("p a d -> p (a d)") if T.loop else X[:, at, :]

            def key_high(T, d):
                s = T.slot(d)
                if T.has(d - PW):
                    need(act, k_out[s], T.slot_count(d - PW, 16))
                need(act, kr_in[s], T.slot_count(d, 16))
                nc.scalar.copy(KS[:, s, 0], KR[:, s]).then_inc(k_high, 1)

            def normalise1(T, d):
                s = T.slot(d)
                hold(act, ACT_H, ln1, T.count(d - 2, 4, 0))
                hold(act, ACT_H, rstd1, T.count(d, 2, 2))
                nc.scalar.activation(XN[:, s], x_at(T, d), ACT.Identity, scale=RS1[:, s, 0:1], bias=RS1[:, s, 1:2]
                                     ).then_inc(norm1, 1)
                if T.has(d - PW):
                    need(act, q_out[s], T.slot_count(d - PW, 16))
                need(act, norm1, T.count(d, 2, 1))
                nc.scalar.copy(QS[:, s, 0], XN[:, s]).then_inc(norm1, 1)

            def normalise2(T):
                s = T.slot(-3)
                if T.has(-6):
                    hold(act, ACT_H, dispatched[s], T.slot_count(-6, 16 * K8))
                hold(act, ACT_H, rstd2, T.count(-3, 2, 2))
                nc.scalar.activation(XN2[:, s, 0:D], x_at(T, -3), ACT.Identity, scale=RS2[:, s, 0:1], bias=RS2[:, s, 1:2]
                                     ).then_inc(norm2, 1)

            def max_high(T, d, h):
                need(act, max_in[h], T.count(d, 32, 0))
                need(act, misc_a if h else misc_b, T.count(0, 1, 0 if h else 1))
                nc.scalar.copy(MXT[:, h, 0, :], MISC_MAX).then_inc(mxt_high, 1)

            act.wait_ge(dve_const, 1)
            nc.scalar.copy(K[0:MAXR, 0].rearrange("p n d -> p (n d)"),
                           bass.AP(ZERO[:, :].tensor, 0, [[D, MAXR], [0, HPT], [1, D]])).then_inc(k_zero, 1)
            for n in range(2):
                key_high(Turn(0, 0), n)
            for n in range(2):
                normalise1(Turn(0, 0), n)

            def turn(T):
                for u in range(UNITS):
                    if T.has(-1):
                        for a in range(2):
                            n = 2 * u + a
                            h = HPT * (T.b - 1) + n
                            if n % 4 == 0:
                                need(act, pv_done, T.count(-1, J, n // 4 - EXP_RING // 4 + 1))
                            need(act, st_done, T.count(-1, HPT, n + 1))
                            nc.scalar.activation(PE_T[:, h % EXP_RING, :], ST[:, h % 2, :], ACT.Exp,
                                                 scale=SCALE).then_inc(exp_done, 1)
                    if u == 0:
                        if T.has(-1):
                            max_high(T, -1, 1)
                        if T.has(-4):
                            s = T.slot(-4)
                            need(act, misc_a, T.count(0, 1, 0))
                            nc.scalar.copy(XT2[:, s], MISC_XT).then_inc(xt_copied, 1)
                    if u == 1 and ahead(T):
                        key_high(T, 2)
                    if u == 3 and ahead(T):
                        normalise1(T, 2)
                    if u == 4 and T.has(0):
                        max_high(T, 0, 0)
                    if u == 5 and T.has(-4):
                        s = T.slot(-4)
                        need(act, route, T.count(-4, 8, 1))
                        nc.scalar.activation(EX[:, s], MISC_E, ACT.Exp, bias=NM[:, s],
                                             accum_out=SE[:, s]).then_inc(rexp, 1)
                    if u == 6 and T.has(-3):
                        normalise2(T)
                    if u % 2 == 0:
                        d, j = (-2, 2 + u // 2) if u < 4 else (-1, (u - 4) // 2)
                        if T.has(d):
                            s = T.slot(d)
                            if j == 0:
                                if T.loop or T.b + d - PW >= 0:
                                    need(act, o_out[s], T.slot_count(d - PW, 16))
                            need(act, pv_done, T.count(d, J, j + 1))
                            nc.scalar.copy(O4[:, s, j, :], OX[:, 0:D]).then_inc(o_copied, 1)

            turns(act, turn)

            act.wait_ge(tab_dve, TAB_OPS)
            over = act.value_load(TAB[0:1, TAB_N - 1:TAB_N], min_val=0, max_val=NO)

            def high_rows(i, n):
                e, b = i * SLOTS + n, n % 2
                if not (isinstance(i, int) and e < 2):
                    need(act, gu_ps, e - 1)
                need(act, xt_ps, e + 1)
                nc.scalar.copy(XTP[:, b, 0], XP).then_inc(xt_high, 1)

            def high_weights(i, n):
                e, w = i * SLOTS + n, n % WS
                if not (isinstance(i, int) and e < WS):
                    need(act, y_ps, e - WS + 1)
                need(act, w_in[n % SLOTS], (i + n // SLOTS) * 16 + 16)
                nc.scalar.copy(WP[:, w, 0], W[:, n % SLOTS, :]).then_inc(w_high, 1)

            def gate(i, n):
                e, b = i * SLOTS + n, n % 2
                if not (isinstance(i, int) and e < 2):
                    need(act, h_done, e - 1)
                need(act, gu_ps, e + 1)
                nc.scalar.activation(SG[:, b, :], GU[:, b, 0, :], ACT.Silu).then_inc(silu_done, 1)

            def high_hidden(i, n):
                e, b = i * SLOTS + n, n % 2
                if not (isinstance(i, int) and e < 2):
                    need(act, y_ps, e - 1)
                need(act, h_done, e + 1)
                nc.scalar.copy(HP[:, b, 0], HT[:, b, :]).then_inc(h_high, 1)

            def weighted(i, n):
                e, b = i * SLOTS + n, n % 2
                need(act, y_ps, e + 1)
                for j in range(NJ):
                    if not (isinstance(i, int) and e < 2):
                        need(act, *added_up_to(i, n - 2, j))
                    m = ROWS_J[j]
                    nc.scalar.activation(Y[0:m, b, j, :], YP[j][0:m], ACT.Copy,
                                         scale=XE[0:m, n % SLOTS, j, bass.ds(e + D, 1)]).then_inc(y_weighted, 1)

            def expert_step(i, n):
                gate(i, n)
                if more(i, n + 2):
                    high_rows(i, n + 2)
                high_hidden(i, n)
                if more(i, n + 2):
                    high_weights(i, n + 2)
                if not (isinstance(i, int) and i == 0 and n == 0):
                    weighted(i, n - 1)

            for n in range(2):
                high_rows(0, n)
                high_weights(0, n)
            for n in range(SLOTS):
                expert_step(0, n)
            with act.Fori(1, E // SLOTS - 1) as i:
                for n in range(SLOTS):
                    expert_step(i, n)
            for n in range(SLOTS):
                expert_step(E // SLOTS - 1, n)
            weighted(E // SLOTS - 1, SLOTS - 1)

            with act.If(over > 0):
                with act.Fori(0, NO) as i:
                    need(act, o_xt_ps, i + 1)
                    nc.scalar.copy(XET[:, 0, :, 0:P], XP[:, :, 0:P]).then_inc(o_xet, 1)
                    need(act, o_gu_ps, i + 1)
                    nc.scalar.activation(SG[:, 0, 0:P], GU[:, 0, 0, 0:P], ACT.Silu).then_inc(o_silu, 1)

            with act.Fori(0, TILES // FS) as i:
                for h in range(FS // 2):
                    hold(act, ACT_H, summed, (i * FS + (2 * h + 2)) * NS)
                    act.dma_start(out[bass.ds((i * FS + 2 * h) * P, 2 * P), :].rearrange("(a p) d -> p a d", p=P),
                                  OT[:, 2 * h:2 * h + 2, :]).then_inc(stored[h], 16)

        @block.tensor
        def _(pe):
            pe.wait_ge(pool_const, 14)
            pe.wait_ge(dve_const, 7)

            def misc_read(T, d, early):
                if early:
                    if T.has(d - 1):
                        need(pe, mxt_low, T.count(d - 1, 2, 2))
                    if T.has(d - 4):
                        need(pe, xt_copied, T.count(d - 4, 1, 1))
                    if T.has(d - 5):
                        need(pe, place, T.count(d - 5, 5, 1))
                else:
                    if T.has(d):
                        need(pe, mxt_low, T.count(d, 2, 1))
                    if T.has(d - 4):
                        need(pe, rexp, T.count(d - 4, 1, 1))

            def step(T, u):
                s0, s1 = T.slot(0), T.slot(-1)
                if T.has(0):
                    if u == 0:
                        if not T.loop and T.b < PW:
                            pe.wait_ge(k_ones, 16)
                        need(pe, k_in[s0], T.slot_count(0, 48))
                        need(pe, q_in[s0], T.slot_count(0, 32))
                    need(pe, max_done, T.count(0, UNITS, u - 1))
                pair = u % 2
                if T.has(0):
                    for a in range(2):
                        n = 2 * u + a
                        for r in range(MT):
                            mm = nc.tensor.matmul(SC[:, pair, a, r * D:(r + 1) * D],
                                                  Q[0:MAXR, s0, n, r * P:(r + 1) * P], K[0:MAXR, s0, n, :],
                                                  start=True, stop=True)
                    mm.then_inc(scored, 1)
                if T.has(-1):
                    if u % 4 == 0:
                        need(pe, max_in[u // 4], T.count(-1, 32, 32))
                    for a in range(2):
                        n = 2 * u + a
                        bank = n % 2
                        need(pe, exp_done, T.count(-1, HPT, n - 1))
                        for r in range(MT):
                            mm = nc.tensor.matmul(ST[:, bank, r * D:(r + 1) * D],
                                                  K[:, s1, n, r * P:(r + 1) * P], Q[:, s1, n, :],
                                                  start=True, stop=True)
                        mm.then_inc(st_done, 1)

            def sums(T, d, j):
                s = T.slot(d)
                if j == 0:
                    need(pe, v_in[s], T.slot_count(d, 16))
                need(pe, exp_done, T.count(d, HPT, 4 * j + 4))
                need(pe, o_copied, T.count(d, J, j))
                for r in range(MT):
                    for g in range(G):
                        h = HPT * (T.b + d) + 4 * j + g
                        c = (4 * j + g) * VC
                        mm = nc.tensor.matmul(OX[32 * g:32 * g + 32, 0:D], V[:, s, r, c:c + 32],
                                              PE_T[:, h % EXP_RING, r * D:(r + 1) * D],
                                              start=(r == 0), stop=(r == 1))
                mm.then_inc(pv_done, 1)

            def ma(T):
                if not (T.has(-1) or T.has(-4) or T.has(-5)):
                    return
                misc_read(T, -1, False)
                if T.has(-1):
                    need(pe, max_done, T.count(-1, UNITS, UNITS))
                    mm = nc.tensor.transpose(MISC_MAX, MX[:, 1, :], IDENT[:, :])
                if T.has(-5):
                    s = T.slot(-5)
                    need(pe, route, T.count(-5, 8, 8))
                    nc.tensor.matmul(MISC_E, UPPER[:, :], MASK[:, s], start=True, stop=False)
                    mm = nc.tensor.matmul(MISC_E, ONES[:, :], SEEN[:, s], start=False, stop=True)
                if T.has(-4):
                    s = T.slot(-4)
                    need(pe, norm2, T.count(-4, 1, 1))
                    for k in range(MT):
                        mm = nc.tensor.transpose(MISC_XT[:, k * P:(k + 1) * P], XN2[:, s, k * P:(k + 1) * P],
                                                 IDENT[:, :])
                mm.then_inc(misc_a, 1)

            def mb(T):
                if not (T.has(0) or T.has(-4)):
                    return
                misc_read(T, 0, True)
                if T.has(0):
                    need(pe, max_done, T.count(0, UNITS, 4))
                    mm = nc.tensor.transpose(MISC_MAX, MX[:, 0, :], IDENT[:, :])
                if T.has(-4):
                    s = T.slot(-4)
                    if not T.loop and T.b == 4:
                        pe.wait_ge(router_in, 16)
                    need(pe, xt_copied, T.count(-4, 1, 1))
                    for k in range(MT):
                        mm = nc.tensor.matmul(MISC_E, XT2[:, s, k * P:(k + 1) * P], RW[:, k, :],
                                              start=(k == 0), stop=(k == MT - 1))
                mm.then_inc(misc_b, 1)

            def turn(T):
                for u in range(UNITS):
                    step(T, u)
                    if u == 0:
                        ma(T)
                    if u == 4:
                        mb(T)
                    if u == 1 and T.has(-2):
                        sums(T, -2, 3)
                    if u in (3, 5, 7) and T.has(-1):
                        sums(T, -1, (u - 3) // 2)

            turns(pe, turn)

            last = TILES % PW
            pe.wait_ge(route, 8 * TILES)
            pe.wait_ge(place, 5 * TILES)
            nc.tensor.matmul(SC[0:E, 0, 0, 0:1], SEEN[:, last], ONES[:, 0:1], start=True, stop=True
                             ).then_inc(tab_pe, 1)
            pe.wait_ge(tab_dve, 6)
            nc.tensor.matmul(SC[0:E, 0, 1, 0:1], UPPER[0:E, 0:E], NTB[:, :], start=True, stop=True
                             ).then_inc(tab_pe, 1)
            pe.wait_ge(tab_dve, TAB_OPS - 3)
            nc.tensor.matmul(SC[0:1, 1, 0, 0:TAB_N], ONESF[:, 0:1], TB[:, :], start=True, stop=True
                             ).then_inc(tab_pe, 1)
            pe.wait_ge(tab_dve, TAB_OPS)
            over = pe.value_load(TAB[0:1, TAB_N - 1:TAB_N], min_val=0, max_val=NO)

            def rows_t(i, n):
                e, s = i * SLOTS + n, n % SLOTS
                need(pe, xe_in[s], (i + n // SLOTS) * 32 + 32)
                if not (isinstance(i, int) and e < 1):
                    need(pe, xt_low, e)
                for k in range(MT):
                    for j, m in enumerate(ROWS_J):
                        mm = nc.tensor.transpose(XP[:, k, j * P:j * P + m], XE[0:m, s, j, k * P:(k + 1) * P],
                                                 IDENT[0:m, 0:m])
                mm.then_inc(xt_ps, 1)

            def gate_up(i, n):
                e, b = i * SLOTS + n, n % 2
                need(pe, xt_low, e + 1)
                need(pe, w_low, e + 1)
                if not (isinstance(i, int) and e < 2):
                    need(pe, h_done, e - 1)
                for c in range(2):
                    steps = [(k, a) for k in range(MT) for a in PRODUCTS]
                    for at, (k, (wa, xa)) in enumerate(steps):
                        mm = nc.tensor.matmul(GU[:, b, c, :],
                                              WP[:, n % WS, wa, k * 2 * I + c * I:k * 2 * I + (c + 1) * I],
                                              XTP[:, b, xa, k, :], start=(at == 0), stop=(at == len(steps) - 1))
                mm.then_inc(gu_ps, 1)

            def down(i, n):
                e, b = i * SLOTS + n, n % 2
                need(pe, h_low, e + 1)
                if not (isinstance(i, int) and e < 1):
                    need(pe, y_weighted, e * NJ)
                for j, m in enumerate(ROWS_J):
                    for at, (ha, wa) in enumerate(PRODUCTS):
                        mm = nc.tensor.matmul(YP[j][0:m], HP[:, b, ha, j * P:j * P + m], WP[:, n % WS, wa, 4 * I:],
                                              start=(at == 0), stop=(at == len(PRODUCTS) - 1))
                mm.then_inc(y_ps, 1)

            def expert_step(i, n):
                gate_up(i, n)
                if more(i, n + 2):
                    rows_t(i, n + 2)
                if not (isinstance(i, int) and i == 0 and n == 0):
                    down(i, n - 1)

            for n in range(2):
                rows_t(0, n)
            for n in range(SLOTS):
                expert_step(0, n)
            with pe.Fori(1, E // SLOTS - 1) as i:
                for n in range(SLOTS):
                    expert_step(i, n)
            for n in range(SLOTS):
                expert_step(E // SLOTS - 1, n)
            down(E // SLOTS - 1, SLOTS - 1)

            with pe.If(over > 0):
                with pe.Fori(0, NO) as i:
                    need(pe, o_loaded, i * 32 + 32)
                    for k in range(MT):
                        mm = nc.tensor.transpose(XP[:, k, 0:P], XE[:, 0, 0, k * P:(k + 1) * P], IDENT[:, :])
                    mm.then_inc(o_xt_ps, 1)
                    need(pe, o_xet, i + 1)
                    for c in range(2):
                        for k in range(MT):
                            mm = nc.tensor.matmul(GU[:, 0, c, 0:P], W[:, 0, k * 2 * I + c * I:k * 2 * I + (c + 1) * I],
                                                  XET[:, 0, k, 0:P], start=(k == 0), stop=(k == MT - 1))
                    mm.then_inc(o_gu_ps, 1)
                    need(pe, o_h, i + 1)
                    nc.tensor.matmul(YP[0], HT[:, 0, 0:P], W[:, 0, 4 * I:], start=True, stop=True).then_inc(o_y_ps, 1)


def kernel(x, ctx_2048, g_xattn, g_ffn, L0_ffn_router_weight, L0_ffn_gate_up_proj, L0_ffn_down_proj):
    import numpy as np
    import concourse.bacc as bacc
    from concourse.bass_utils import run_bass_kernel_spmd as run

    f = np.float32

    def tiles(a):
        return np.ascontiguousarray(a).reshape(TILES, HPT, HR, D).transpose(0, 2, 1, 3).reshape(TILES, P, D)

    rows = tiles(x).reshape(TOK, D)
    keys = np.zeros((TILES + 3, P, D), f)
    keys[:TILES] = tiles(ctx_2048)
    vals = np.ones((TILES + 1, P, MT, VW), f)
    ctx_t = np.ascontiguousarray(ctx_2048).reshape(TILES, HPT, HR, MT, P).transpose(0, 4, 3, 1, 2)
    heads = np.ones((TILES, P, MT, HPT, VC), f)
    heads[..., :HR] = ctx_t
    vals[:TILES, :, :, :HPT * VC] = heads.reshape(TILES, P, MT, HPT * VC)
    gu = np.ascontiguousarray(L0_ffn_gate_up_proj).reshape(E, 2 * I, MT, P).transpose(0, 3, 2, 1).reshape(E, P, 4 * I)
    dn = np.ascontiguousarray(L0_ffn_down_proj).transpose(0, 2, 1)
    arrays = {
        "x_in_dram": rows,
        "keys_dram": keys,
        "vals_dram": vals,
        "g_attn_dram": np.ascontiguousarray(g_xattn).reshape(1),
        "g_ffn_dram": np.ascontiguousarray(g_ffn).reshape(1),
        "router_dram": np.ascontiguousarray(np.asarray(L0_ffn_router_weight).T),
        "experts_dram": np.ascontiguousarray(np.concatenate([gu, dn], axis=2)),
    }
    nc = bacc.Bacc("TRN2", target_bir_lowering=False, num_devices=1)
    aps = [nc.dram_tensor(n, a.shape, F32, kind="ExternalInput").ap() for n, a in arrays.items()]
    out = nc.dram_tensor("out_dram", (TOK, D), F32, kind="ExternalOutput").ap()
    build(nc, *aps, out)
    r = run(nc, [arrays], core_ids=[0])
    got = r.results[0]["out_dram"].reshape(TILES, HR, HPT, D).transpose(0, 2, 1, 3)
    return np.ascontiguousarray(got).reshape(B, S, D)
```
